# Optimizing a Trainium2 kernel written in Bass

```python
import numpy as np
import jax
import jax.numpy as jnp

def _softmax(x, axis=-1):
    return jax.nn.softmax(x, axis=axis)

def _gelu(x):
    return jax.nn.gelu(x, approximate=True)

def _silu(x):
    return jax.nn.silu(x)

def _sigmoid(x):
    return jax.nn.sigmoid(x)

def _layernorm(x, axis=-1, eps=1e-05):
    m = jnp.mean(x, axis=axis, keepdims=True)
    v = jnp.var(x, axis=axis, keepdims=True)
    return (x - m) / jnp.sqrt(v + eps)

def _scatter_add(tgt, idx, src, axis=0):
    return tgt.at[idx].add(src)

def _segment_sum(src, seg, n):
    return jax.ops.segment_sum(src, seg, n)
kernel_name = 'mk_sandwich_d1_jaxref_r8_11794c'

def setup_inputs(seed: int=0):
    np.random.seed(seed)
    _w = jnp.asarray

    def _L0_attn_setup():
        import jax, jax.numpy as jnp
        import numpy as np
        DIM = 128
        DIM_HEAD = 64
        HEADS = DIM // DIM_HEAD
        SCALE = DIM_HEAD ** (-0.5)
        RMS_EPS = 1e-08
        LN_EPS = 1e-05

        def _layernorm(x, g, b):
            mu = jnp.mean(x, axis=-1, keepdims=True)
            var = jnp.mean(jnp.square(x - mu), axis=-1, keepdims=True)
            return (x - mu) * jax.lax.rsqrt(var + LN_EPS) * g + b

        def _rmsnorm(x, gamma):
            norm = jnp.sqrt(jnp.sum(jnp.square(x), axis=-1, keepdims=True)) * DIM_HEAD ** (-0.5)
            return x / jnp.maximum(norm, RMS_EPS) * gamma
        key = jax.random.key(seed)
        ks = jax.random.split(key, 8)
        b, n = (2, 256)
        x = jax.random.normal(ks[0], (b, n, DIM), dtype=jnp.float32)
        init = 1.0 / np.sqrt(DIM)
        Wq = jax.random.uniform(ks[1], (DIM, DIM), jnp.float32, -init, init)
        Wk = jax.random.uniform(ks[2], (DIM, DIM), jnp.float32, -init, init)
        Wv = jax.random.uniform(ks[3], (DIM, DIM), jnp.float32, -init, init)
        Wo = jax.random.uniform(ks[4], (DIM, DIM), jnp.float32, -init, init)
        bo = jax.random.uniform(ks[5], (DIM,), jnp.float32, -init, init)
        ln_g = jnp.ones((DIM,), jnp.float32)
        ln_b = jnp.zeros((DIM,), jnp.float32)
        q_gamma = jnp.ones((DIM_HEAD,), jnp.float32)
        k_gamma = jnp.ones((DIM_HEAD,), jnp.float32)
        return dict(x=x, Wq=Wq, Wk=Wk, Wv=Wv, Wo=Wo, bo=bo, ln_g=ln_g, ln_b=ln_b, q_gamma=q_gamma, k_gamma=k_gamma)
    _L0_attn_in = _L0_attn_setup()

    def _L0_ffn_setup():
        import jax, jax.numpy as jnp
        import numpy as np
        D_MODEL = 128
        D1, D2 = (32, 32)
        F1, F2 = (64, 64)
        E = 64
        TOP_K = 2

        def kmoe(x_flat, W_router, A, B, scale, bias, d_in1, d_in2, d_out1, d_out2, top_k):
            logits = x_flat @ W_router.T
            vals, idx = jax.lax.top_k(logits, top_k)
            probs = jax.nn.softmax(vals, axis=-1)
            xs = x_flat.reshape(-1, d_in1, d_in2)
            Ag = A[idx]
            Bg = B[idx]
            Y = jnp.einsum('nkoi,nij,nkpj->nkop', Ag, xs, Bg)
            out = jnp.einsum('nkop,nk->nop', Y, probs).reshape(-1, d_out1 * d_out2)
            return out * scale + bias
        key = jax.random.key(seed)
        ks = jax.random.split(key, 12)
        s = 0.02
        return {'x': jax.random.normal(ks[0], (4, 256, D_MODEL), dtype=jnp.float32), 'W_up': jax.random.normal(ks[1], (E, D1 * D2), dtype=jnp.float32) * s, 'A_up': jax.random.normal(ks[2], (E, F1, D1), dtype=jnp.float32) * s, 'B_up': jax.random.normal(ks[3], (E, F2, D2), dtype=jnp.float32) * s, 'scale_up': jnp.ones((1,), dtype=jnp.float32), 'bias_up': jnp.zeros((F1 * F2,), dtype=jnp.float32), 'W_down': jax.random.normal(ks[4], (E, F1 * F2), dtype=jnp.float32) * s, 'A_down': jax.random.normal(ks[5], (E, D1, F1), dtype=jnp.float32) * s, 'B_down': jax.random.normal(ks[6], (E, D2, F2), dtype=jnp.float32) * s, 'scale_down': jnp.ones((1,), dtype=jnp.float32), 'bias_down': jnp.zeros((D1 * D2,), dtype=jnp.float32)}
    _L0_ffn_in = _L0_ffn_setup()
    _d = {'L0_attn_x': _L0_attn_in['x'], 'L0_attn_Wq': _L0_attn_in['Wq'], 'L0_attn_Wk': _L0_attn_in['Wk'], 'L0_attn_Wv': _L0_attn_in['Wv'], 'L0_attn_Wo': _L0_attn_in['Wo'], 'L0_attn_bo': _L0_attn_in['bo'], 'L0_attn_ln_g': _L0_attn_in['ln_g'], 'L0_attn_ln_b': _L0_attn_in['ln_b'], 'L0_attn_q_gamma': _L0_attn_in['q_gamma'], 'L0_attn_k_gamma': _L0_attn_in['k_gamma'], 'L0_ffn_W_up': _L0_ffn_in['W_up'], 'L0_ffn_A_up': _L0_ffn_in['A_up'], 'L0_ffn_B_up': _L0_ffn_in['B_up'], 'L0_ffn_scale_up': _L0_ffn_in['scale_up'], 'L0_ffn_bias_up': _L0_ffn_in['bias_up'], 'L0_ffn_W_down': _L0_ffn_in['W_down'], 'L0_ffn_A_down': _L0_ffn_in['A_down'], 'L0_ffn_B_down': _L0_ffn_in['B_down'], 'L0_ffn_scale_down': _L0_ffn_in['scale_down'], 'L0_ffn_bias_down': _L0_ffn_in['bias_down']}
    _x0 = _d['L0_attn_x']
    _d['L0_attn_x'] = jax.random.normal(jax.random.fold_in(jax.random.key(seed), 1), (8, 1024, 128), dtype=_x0.dtype)
    del _x0
    return _d

def reference(L0_attn_x, L0_attn_Wq, L0_attn_Wk, L0_attn_Wv, L0_attn_Wo, L0_attn_bo, L0_attn_ln_g, L0_attn_ln_b, L0_attn_q_gamma, L0_attn_k_gamma, L0_ffn_W_up, L0_ffn_A_up, L0_ffn_B_up, L0_ffn_scale_up, L0_ffn_bias_up, L0_ffn_W_down, L0_ffn_A_down, L0_ffn_B_down, L0_ffn_scale_down, L0_ffn_bias_down):

    def _L0_attn_ref(x, Wq, Wk, Wv, Wo, bo, ln_g, ln_b, q_gamma, k_gamma):
        import jax, jax.numpy as jnp
        import numpy as np
        DIM = 128
        DIM_HEAD = 64
        HEADS = DIM // DIM_HEAD
        SCALE = DIM_HEAD ** (-0.5)
        RMS_EPS = 1e-08
        LN_EPS = 1e-05

        def _layernorm(x, g, b):
            mu = jnp.mean(x, axis=-1, keepdims=True)
            var = jnp.mean(jnp.square(x - mu), axis=-1, keepdims=True)
            return (x - mu) * jax.lax.rsqrt(var + LN_EPS) * g + b

        def _rmsnorm(x, gamma):
            norm = jnp.sqrt(jnp.sum(jnp.square(x), axis=-1, keepdims=True)) * DIM_HEAD ** (-0.5)
            return x / jnp.maximum(norm, RMS_EPS) * gamma
        b, n, _ = x.shape
        xn = _layernorm(x, ln_g, ln_b)

        def split_heads(t):
            return t.reshape(b, n, HEADS, DIM_HEAD).transpose(0, 2, 1, 3)
        q = split_heads(xn @ Wq.T)
        k = split_heads(xn @ Wk.T)
        v = split_heads(xn @ Wv.T)
        q = _rmsnorm(q, q_gamma) * SCALE
        k = _rmsnorm(k, k_gamma)
        sim = jnp.einsum('bhid,bhjd->bhij', q, k)
        attn = jax.nn.softmax(sim, axis=-1)
        out = jnp.einsum('bhij,bhjd->bhid', attn, v)
        out = out.transpose(0, 2, 1, 3).reshape(b, n, DIM)
        return out @ Wo.T + bo

    def _L0_ffn_ref(x, W_up, A_up, B_up, scale_up, bias_up, W_down, A_down, B_down, scale_down, bias_down):
        import jax, jax.numpy as jnp
        import numpy as np
        D_MODEL = 128
        D1, D2 = (32, 32)
        F1, F2 = (64, 64)
        E = 64
        TOP_K = 2

        def kmoe(x_flat, W_router, A, B, scale, bias, d_in1, d_in2, d_out1, d_out2, top_k):
            logits = x_flat @ W_router.T
            vals, idx = jax.lax.top_k(logits, top_k)
            probs = jax.nn.softmax(vals, axis=-1)
            xs = x_flat.reshape(-1, d_in1, d_in2)
            Ag = A[idx]
            Bg = B[idx]
            Y = jnp.einsum('nkoi,nij,nkpj->nkop', Ag, xs, Bg)
            out = jnp.einsum('nkop,nk->nop', Y, probs).reshape(-1, d_out1 * d_out2)
            return out * scale + bias
        orig_shape = x.shape
        x_flat = x.reshape(-1, D1 * D2)
        h = kmoe(x_flat, W_up, A_up, B_up, scale_up, bias_up, D1, D2, F1, F2, TOP_K)
        h = jax.nn.gelu(h, approximate=False)
        y = kmoe(h, W_down, A_down, B_down, scale_down, bias_down, F1, F2, D1, D2, TOP_K)
        return y.reshape(*orig_shape[:-1], D_MODEL)
    x = L0_attn_x
    x = x + _layernorm(_L0_attn_ref(_layernorm(x, axis=-1), L0_attn_Wq, L0_attn_Wk, L0_attn_Wv, L0_attn_Wo, L0_attn_bo, L0_attn_ln_g, L0_attn_ln_b, L0_attn_q_gamma, L0_attn_k_gamma), axis=-1)
    x = x + _layernorm(_L0_ffn_ref(_layernorm(x, axis=-1), L0_ffn_W_up, L0_ffn_A_up, L0_ffn_B_up, L0_ffn_scale_up, L0_ffn_bias_up, L0_ffn_W_down, L0_ffn_A_down, L0_ffn_B_down, L0_ffn_scale_down, L0_ffn_bias_down), axis=-1)
    return x

_drawn_inputs = setup_inputs


def setup_inputs(seed=0):
    import zlib

    import numpy as np

    out = dict(_drawn_inputs(seed))
    spreads = {'L0_attn_ln_g': (1.0, 0.2),
     'L0_attn_ln_b': (0.0, 0.1),
     'L0_attn_q_gamma': (1.0, 0.2),
     'L0_attn_k_gamma': (1.0, 0.2),
     'L0_ffn_bias_up': (0.0, 0.8),
     'L0_ffn_bias_down': (0.0, 0.1)}
    factors = {'L0_ffn_W_up': 8.0,
     'L0_ffn_A_up': 8.0,
     'L0_ffn_B_up': 8.0,
     'L0_ffn_W_down': 8.0,
     'L0_ffn_A_down': 8.0,
     'L0_ffn_B_down': 8.0}
    for name, (base, spread) in spreads.items():
        noise = np.random.default_rng([zlib.crc32(name.encode()), seed]).standard_normal(out[name].shape)
        drawn = base * np.exp(spread * noise) if base else spread * noise
        out[name] = jnp.asarray(drawn.astype(out[name].dtype))
    for name, factor in factors.items():
        out[name] = (out[name] * factor).astype(out[name].dtype)
    return out
```

```python
from contextlib import ExitStack

import numpy as np

import concourse.bass as bass
from concourse import mybir

ALU = mybir.AluOpType
ACT = mybir.ActivationFunctionType
AX = mybir.AxisListType
F32 = mybir.dt.float32
F16 = mybir.dt.float16
BF16 = mybir.dt.bfloat16
I32 = mybir.dt.int32
U32 = mybir.dt.uint32

P = 128
B, N, C = 8, 1024, 128
HEADS, DH = 2, 64
T = N // P
E = 64
D1, F1 = 32, 64
G = P // 2
BANK = 512
QH = N // BANK
UNITS = HEADS * QH
EPS = 1e-5
RMS_FLOOR = 1e-16
EXP_TOP = 80.0


class Count:

    def __init__(self, eng, sem):
        self.eng, self.sem, self.n = eng, sem, 0

    def __call__(self, instruction):
        self.n += 1
        return instruction.then_inc(self.sem, 1)

    def settle(self):
        self.eng.wait_ge(self.sem, self.n)

    def then(self, instruction):
        self(instruction)
        self.settle()


FFN_FILLS = [
    ("xt", 2, "D"), ("logits", 1, "D"), ("route", 1, "D"),
    ("gather_b", 8, "A"), ("stage1", 8, "D"), ("gather_a", 8, "A"), ("stage2", 8, "D"),
    ("dlogits", 2, "D"), ("droute", 1, "D"),
    ("dgather_a", 8, "A"), ("dgather_b", 8, "A"), ("dstage1", 8, "D"), ("dstage2", 2, "A"),
]
FILL_AT, FILL_BY = {}, []
for _name, _n, _by in FFN_FILLS:
    FILL_AT[_name] = len(FILL_BY)
    FILL_BY += [_by] * _n


def evacuated_by(engine, fill):
    return FILL_BY[:fill + 1].count(engine)


def build_program(nc, x, w_qkv, w_o, bo, ln_gamma, tables, w_up, w_down, bias_up, bias_down, scales, shape_consts, out):
    with ExitStack() as ctx:
        def sb(name, shape, dt=F32):
            return ctx.enter_context(nc.sbuf_tensor(name, shape, dt))

        wqkv = sb("wqkv", [P, 3 * C])
        wo = sb("wo", [P, C])
        bo_rows = sb("bo_rows", [P, C])
        gam = sb("gam", [P, 4])
        wup = sb("wup", [P, T, E])
        wdn = sb("wdn", [P, F1, E])
        bup = sb("bup", [P, F1])
        bdn = sb("bdn", [P, N])
        scl = sb("scl", [P, 2])
        tab = [sb(f"tab{i}", [P, 2048], F16) for i in range(4)]
        unscale = sb("unscale", [P, 4])
        cst = sb("cst", [P, 3 * P + G + 1])
        ident, iota = cst[:, 0:P], cst[:, P:2 * P]
        mask_half, mask_g = cst[:, 2 * P:3 * P], cst[:, 3 * P:3 * P + G]
        mask_low = cst[:, 3 * P + G:3 * P + G + 1]
        shift = sb("shift", [P, 2])

        xin = sb("xin", [P, T, C])
        xn = sb("xn", [P, T, C])
        xnT = sb("xnT", [P, T * P])
        qk = sb("qk", [P, T, 2 * C])
        vv = sb("vv", [P, T, HEADS, DH + 1])
        qT = sb("qT", [P, N])
        kT = sb("kT", [P, N])
        pT = sb("pT", [P, 2, T, BANK])
        sq = pT[:, 0, 0:4, :].rearrange("p a b -> p (a b)").rearrange("p (t c) -> p t c", t=T)
        attn = qk[:, 0:4, :].rearrange("p a b -> p (a b)").rearrange("p (t c) -> p t c", t=T)
        y = qk[:, 4:8, :].rearrange("p a b -> p (a b)").rearrange("p (t c) -> p t c", t=T)
        attnT = xnT

        x2 = sb("x2", [P, T, C])
        x2n = sb("x2n", [P, T, C])
        ydn = x2n
        xt = sb("xt", [P, T, P])
        ys = xt[:, :, :].rearrange("p a b -> p (a b)")
        res = xt
        xbd = sb("xbd", [P, G, P])
        stage = xbd[:, :, :].rearrange("p a b -> p (a b)").rearrange("p (i n) -> p i n", i=4)
        gb = sb("gb", [P, G, F1])
        ga = sb("ga", [P, G, F1])
        tok = sb("tok", [P, G, F1])
        lg = sb("lg", [P, E])
        m8 = sb("m8", [P, 8])
        i8 = sb("i8", [P, 8], U32)
        idx = sb("idx", [P, 2])
        gap = sb("gap", [P, 4])
        prob = sb("prob", [P, 2])
        oh = sb("oh", [P, 2, P])
        spread = sb("spread", [P, 2 * P])
        ohA = sb("ohA", [P, 2, P], BF16)
        ohB = sb("ohB", [P, 2, P], BF16)
        pb = sb("pb", [P, P])

        bn = sb("bn", [P, T, 6])
        mv = sb("mv", [P, T, 2])
        rs = sb("rs", [P, 4 * T])
        rt = sb("rt", [P, 4 * T])
        rv = sb("rv", [P, 4 * T])
        rden = sb("rden", [P, 4])
        ms = sb("ms", [P, 4])
        bits = sb("bits", [P, 2], I32)

        banks = [ctx.enter_context(nc.psum_tensor(f"bank{i}", [P, BANK], F32)) for i in range(8)]

        def sem(name):
            return ctx.enter_context(nc.semaphore(name))

        s_const, s_tab, s_setup = sem("weights_loaded"), sem("tables_loaded"), sem("setup_done")
        s_setchain, s_bound, s_bound_all = sem("setup_chain"), sem("bound_ready"), sem("bound_spread")
        s_done, s_go = sem("engines_done"), {k: sem(f"go_{k}") for k in ("sp", "act", "pe", "dve")}
        names = ["xnorm_ready", "att_filled", "xnT_by_act", "xnT_by_dve", "qkv_by_act", "qkv_by_dve", "squares_ready",
                 "qk_scaled", "qkT_by_act", "qkT_by_dve", "scores_filled", "probs_ready", "pv_filled", "attn_ready",
                 "attnT_by_act", "attnT_by_dve", "y_ready", "x2_ready", "x2n_ready",
                 "ffn_filled", "ffn_by_A", "ffn_by_D", "xbd_ready", "gap_ready", "gap_exp", "hidden_summed",
                 "hidden_ready", "route_ready", "ys_stored", "y_loaded", "ydn_in", "out_ready", "out_stored", "x_loaded",
                 "dve_chain", "act_chain", "ones_ready"]
        S = {n: sem(n) for n in names}
        nums = sorted(S[n].num for n in names)
        assert nums == list(range(nums[0], nums[0] + len(names)))

        scratch = nc.dram_tensor("y_scratch", [P, N], F32).ap()
        x_v = x.rearrange("b (p t) c -> (b p) t c", t=T)
        out_v = out.rearrange("b (p t) c -> (b p) t c", t=T)

        block = ctx.enter_context(nc.Block())

        def fill_wait(eng, fill):
            for who in "AD":
                n = evacuated_by(who, fill)
                if n:
                    eng.wait_ge(S[f"ffn_by_{who}"], n)

        @block.sync
        def _(sp):
            loads = [(wqkv[:, :], w_qkv), (wo[:, :], w_o), (bo_rows[:, :], bo), (gam[:, :], ln_gamma),
                     (wup[:, :, :], w_up), (wdn[:, :, :], w_down), (bup[:, :], bias_up), (bdn[:, :], bias_down),
                     (scl[:, :], scales), (cst[:, :], shape_consts)]
            for dst, src in loads:
                sp.dma_start(dst, src).then_inc(s_const, 16)
            for i in range(4):
                for half in range(2):
                    sp.dma_start(stage[half * E:(half + 1) * E, i, :], tables[i]).then_inc(s_tab, 16)

            with sp.Fori(0, B) as b:
                sp.dma_start(xin[:, :, :], x_v[bass.ds(b * P, P)]).then_inc(S["x_loaded"], 16)
                sp.wait_ge(S["ffn_by_A"], evacuated_by("A", FILL_AT["dstage2"] + 1))
                for c in range(4):
                    sp.dma_start(scratch.rearrange("(s c) (o p) -> c o s p", c=4, p=D1)[c],
                                 ys[c * D1:(c + 1) * D1, :].rearrange("o (s p) -> o s p", p=D1)).then_inc(S["ys_stored"], 16)
                sp.wait_ge(S["ys_stored"], 64)
                sp.dma_start(ydn[:, :, :], scratch.rearrange("n (t c) -> n t c", t=T)).then_inc(S["y_loaded"], 16)
                sp.wait_ge(S["out_ready"], 1)
                sp.dma_start(out_v[bass.ds(b * P, P)], res[:, :, :]).then_inc(S["out_stored"], 16)
                sp.wait_ge(S["out_stored"], 16)
                sp.drain().then_inc(s_done, 1)
                sp.wait_ge(s_go["sp"], 1)
                sp.sem_clear(s_go["sp"])

        @block.gpsimd
        def _(pool):
            pool.wait_ge(s_bound, 1)
            nc.gpsimd.partition_all_reduce(shift[:, 1:2], shift[:, 0:1], P, bass.bass_isa.ReduceOp.max).then_inc(s_bound_all, 1)
            with pool.Fori(0, B) as b:
                pool.wait_ge(S["qkv_by_act"], T // 2)
                pool.wait_ge(S["qkv_by_dve"], T // 2)
                nc.gpsimd.tensor_tensor(sq[:, :, :], qk[:, :, :], qk[:, :, :], ALU.mult).then_inc(S["squares_ready"], 1)
                pool.wait_ge(s_done, 4)
                pool.sem_clear(range(nums[0], nums[0] + len(names)))
                pool.sem_clear(s_done)
                for k in ("sp", "act", "pe", "dve"):
                    pool.sem_inc(s_go[k], 1)

        @block.scalar
        def _(act):
            A = nc.scalar
            act.wait_ge(s_const, 160)
            act.wait_ge(s_setup, 1)
            with act.Fori(0, B) as b:
                act.wait_ge(S["att_filled"], 1)
                A.activation(xnT[:, 0:BANK], banks[0][:, :], ACT.Identity, bias=gam[:, 1:2], scale=gam[:, 0:1]).then_inc(S["xnT_by_act"], 1)
                for t in range(0, T, 2):
                    act.wait_ge(S["att_filled"], 3 + t)
                    A.activation(qk[:, t, :], banks[(2 + t) % 4][:, 0:2 * C], ACT.Copy)
                    A.activation(vv[:, t, :, 0:DH], banks[(2 + t) % 4][:, 2 * C:3 * C].rearrange("p (h d) -> p h d", h=HEADS),
                                 ACT.Copy).then_inc(S["qkv_by_act"], 1)
                for f in (0, 2):
                    act.wait_ge(S["att_filled"], 11 + f)
                    dst, col = ((qT, 2), (kT, 3))[f // 2]
                    A.activation(dst[:, 0:BANK], banks[f][:, :], ACT.Copy, scale=gam[:, col:col + 1]).then_inc(S["qkT_by_act"], 1)
                for u in range(UNITS):
                    if u >= 2:
                        act.wait_ge(S["pv_filled"], u - 1)
                    for kt in range(T):
                        act.wait_ge(S["scores_filled"], u * T + kt + 1)
                        A.activation(pT[:, u % 2, kt, :], banks[kt % 2][:, :], ACT.Exp, bias=shift[:, 0:1],
                                     scale=DH ** -0.5).then_inc(S["probs_ready"], 1)
                act.wait_ge(S["att_filled"], 15)
                A.activation(attnT[:, 0:BANK], banks[0][:, :], ACT.Copy).then_inc(S["attnT_by_act"], 1)

                act.wait_ge(S["gap_ready"], 1)
                A.activation(gap[:, 1:2], gap[:, 0:1], ACT.Exp).then_inc(S["gap_exp"], 1)
                act.wait_ge(S["ffn_by_D"], 2)
                for cb in range(4):
                    for c in range(4):
                        i = A.activation(xbd[32 * c:32 * c + 32, :, 32 * c + cb:32 * c + 32:4].rearrange("j g t -> j t g"),
                                         xt[32 * cb:32 * cb + 32, :, G * (c // 2):G * (c // 2) + G], ACT.Copy)
                i.then_inc(S["xbd_ready"], 1)

                def evacuate_gather(stage, i, dst, k_outer):
                    fill = FILL_AT[stage] + i
                    act.wait_ge(S["ffn_filled"], fill + 1)
                    bank = banks[4 + fill % 4]
                    if k_outer:
                        src = bank[:, :].rearrange("q (e k g) -> q e k g", e=4, k=2)
                        to = dst[:, :, :].rearrange("q g (k e) -> q e k g", k=2)[:, 4 * i:4 * i + 4]
                    else:
                        src = bank[:, :].rearrange("q (e g) -> q e g", e=8)
                        to = dst[:, :, :].rearrange("q g e -> q e g")[:, 8 * i:8 * i + 8]
                    if k_outer:
                        for k in range(2):
                            last = A.activation(to[:, :, k], src[:, :, k], ACT.Copy)
                    else:
                        last = A.activation(to, src, ACT.Copy)
                    last.then_inc(S["ffn_by_A"], 1)

                for i in range(8):
                    evacuate_gather("gather_b", i, gb, False)
                for i in range(8):
                    evacuate_gather("gather_a", i, ga, False)
                for i in range(8):
                    act.wait_ge(S["ffn_by_D"], evacuated_by("D", FILL_AT["stage2"] + i))
                    A.activation(tok[:, 8 * i:8 * i + 8, :], tok[:, 8 * i:8 * i + 8, :], ACT.Gelu).then_inc(S["hidden_ready"], 1)
                act.wait_ge(S["gap_ready"], 2)
                A.activation(gap[:, 1:2], gap[:, 0:1], ACT.Exp).then_inc(S["gap_exp"], 1)
                for i in range(8):
                    evacuate_gather("dgather_a", i, gb, True)
                for i in range(8):
                    evacuate_gather("dgather_b", i, ga, True)
                for i in range(2):
                    fill = FILL_AT["dstage2"] + i
                    act.wait_ge(S["ffn_filled"], fill + 1)
                    A.activation(ys[:, BANK * i:BANK * i + BANK], banks[4 + fill % 4][:, :], ACT.Copy).then_inc(S["ffn_by_A"], 1)
                act.drain().then_inc(s_done, 1)
                act.wait_ge(s_go["act"], 1)
                act.sem_clear(s_go["act"])

        @block.vector
        def _(dve):
            V = nc.vector
            setup = Count(dve, s_setchain)
            dve.wait_ge(s_const, 160)
            dve.wait_ge(s_tab, 128)
            for i in range(4):
                setup(V.tensor_reduce(ms[:, 0:1], stage[:, i, :], AX.X, ALU.max))
                setup.then(V.tensor_reduce(ms[:, 1:2], stage[:, i, :], AX.X, ALU.min))
                setup.then(V.scalar_tensor_tensor(out=ms[:, 2:3], in0=ms[:, 1:2], scalar=-1.0, in1=ms[:, 0:1], op0=ALU.mult, op1=ALU.max))
                setup.then(V.tensor_scalar(ms[:, 3:4], ms[:, 2:3], 1e-30, None, ALU.max))
                setup.then(V.tensor_scalar(bits[:, 0:1], ms[:, 3:4].bitcast(I32), 0x7F800000, None, ALU.bitwise_and))
                setup.then(V.tensor_scalar(unscale[:, i:i + 1], bits[:, 0:1].bitcast(F32), 2.0 ** -13, None, ALU.mult))
                setup.then(V.tensor_scalar(bits[:, 1:2], unscale[:, i:i + 1].bitcast(I32), -1, 0x7F000000, ALU.mult, ALU.add))
                setup.then(V.tensor_scalar(stage[:, i, :], stage[:, i, :], bits[:, 1:2].bitcast(F32), None, ALU.mult))
                setup.then(V.tensor_copy(tab[i][:, :], stage[:, i, :]))
                setup.then(V.scalar_tensor_tensor(out=tab[i][:, :], in0=tab[i][:, :], scalar=mask_low, in1=stage[:, i, :],
                                                  op0=ALU.mult, op1=ALU.add))
            setup(V.memset(xbd[:, :, :], 0.0))
            setup(V.memset(vv[:, :, :, DH:DH + 1], 1.0))
            setup.then(V.tensor_tensor(ms[:, 0:1], gam[:, 2:3], gam[:, 3:4], ALU.mult))
            setup.then(V.tensor_scalar(ms[:, 1:2], ms[:, 0:1], -1.0, None, ALU.mult))
            V.tensor_tensor(shift[:, 0:1], ms[:, 0:1], ms[:, 1:2], ALU.max).then_inc(s_bound, 1)
            dve.wait_ge(s_bound_all, 1)
            setup.then(V.tensor_scalar(ms[:, 2:3], shift[:, 1:2], -(DH ** 0.5), EXP_TOP, ALU.mult, ALU.add))
            V.tensor_scalar(shift[:, 0:1], ms[:, 2:3], 0.0, None, ALU.min).then_inc(s_setup, 1)
            dve.wait_ge(s_setup, 1)

            def rsqrt(chain, n):
                chain.then(V.tensor_scalar(rs[:, 0:n].bitcast(I32), rv[:, 0:n].bitcast(I32), -0.5, float(0x5F3759DF), ALU.mult, ALU.add))
                for _ in range(3):
                    chain.then(V.scalar_tensor_tensor(out=rt[:, 0:n], in0=rs[:, 0:n], scalar=-0.5, in1=rs[:, 0:n], op0=ALU.mult, op1=ALU.mult))
                    chain.then(V.tensor_tensor(rt[:, 0:n], rt[:, 0:n], rv[:, 0:n], ALU.mult))
                    chain.then(V.scalar_tensor_tensor(out=rs[:, 0:n], in0=rt[:, 0:n], scalar=1.5, in1=rs[:, 0:n], op0=ALU.add, op1=ALU.mult))

            def normalise(chain, dst, src, twice=False):
                for t in range(T):
                    chain(V.bn_stats(bn[:, t, :], src[:, t, :]))
                chain.settle()
                for t in range(T):
                    chain(V.bn_aggr(mv[:, t, :], bn[:, t, :]))
                chain.settle()
                a, c = (1.0 + EPS, EPS * EPS) if twice else (1.0, EPS)
                chain.then(V.tensor_scalar(rv[:, 0:T], mv[:, :, 1], a, c, ALU.mult, ALU.add))
                rsqrt(chain, T)
                for t in range(T):
                    chain(V.tensor_scalar(dst[:, t, :], src[:, t, :], mv[:, t, 0:1], rs[:, t:t + 1], ALU.subtract, ALU.mult))
                chain.settle()

            def top2(chain, layer):
                chain.then(V.max(m8[:, :], lg[:, :]))
                chain(V.tensor_tensor(gap[:, 0:1], m8[:, 1:2], m8[:, 0:1], ALU.subtract))
                chain(V.max_index(i8[:, :], m8[:, :], lg[:, :]))
                chain.settle()
                V.tensor_copy(idx[:, :], i8[:, 0:2]).then_inc(S["gap_ready"], 1)
                dve.wait_ge(S["gap_ready"], layer + 1)
                for k in range(2):
                    chain(V.tensor_scalar(oh[:, k, :], iota, idx[:, k:k + 1], None, ALU.is_equal))
                dve.wait_ge(S["gap_exp"], layer + 1)
                chain.then(V.tensor_scalar(gap[:, 2:3], gap[:, 1:2], 1.0, None, ALU.add))
                chain.then(V.reciprocal(gap[:, 3:4], gap[:, 2:3]))
                chain.then(V.tensor_tensor(prob[:, 0:1], gap[:, 3:4], scl[:, layer:layer + 1], ALU.mult))
                chain.then(V.tensor_tensor(prob[:, 1:2], gap[:, 1:2], prob[:, 0:1], ALU.mult))

            def filled(stage, i=0):
                fill = FILL_AT[stage] + i
                dve.wait_ge(S["ffn_filled"], fill + 1)
                return banks[4 + fill % 4]

            with dve.Fori(0, B) as b:
                chain = Count(dve, S["dve_chain"])
                dve.wait_ge(S["x_loaded"], 16)
                normalise(chain, xn, xin, twice=True)
                dve.drain().then_inc(S["xnorm_ready"], 1)
                dve.wait_ge(S["att_filled"], 2)
                V.tensor_scalar(xnT[:, BANK:N], banks[1][:, :], gam[:, 0:1], gam[:, 1:2], ALU.mult, ALU.add).then_inc(S["xnT_by_dve"], 1)
                for t in range(1, T, 2):
                    dve.wait_ge(S["att_filled"], 3 + t)
                    V.tensor_copy(qk[:, t, :], banks[(2 + t) % 4][:, 0:2 * C])
                    V.tensor_copy(vv[:, t, :, 0:DH], banks[(2 + t) % 4][:, 2 * C:3 * C].rearrange("p (h d) -> p h d", h=HEADS))\
                        .then_inc(S["qkv_by_dve"], 1)
                dve.wait_ge(S["squares_ready"], 1)
                chain.then(V.tensor_reduce(rt[:, 0:4 * T], sq[:, :, :].rearrange("p t (m d) -> p (t m) d", d=DH), AX.X, ALU.add))
                chain.then(V.tensor_scalar(rv[:, 0:4 * T], rt[:, 0:4 * T], 1.0 / DH, RMS_FLOOR, ALU.mult, ALU.max))
                rsqrt(chain, 4 * T)
                qk_v = qk[:, :, :].rearrange("p t (m d) -> p (t m) d", d=DH)
                V.tensor_tensor(qk_v, qk_v, rs[:, 0:4 * T].unsqueeze(2).broadcast_to([P, 4 * T, DH]), ALU.mult).then_inc(S["qk_scaled"], 1)
                for f in (1, 3):
                    dve.wait_ge(S["att_filled"], 11 + f)
                    dst, col = ((qT, 2), (kT, 3))[f // 2]
                    V.tensor_scalar(dst[:, BANK:N], banks[f][:, :], gam[:, col:col + 1], None, ALU.mult).then_inc(S["qkT_by_dve"], 1)
                for u in range(UNITS):
                    h, qh = divmod(u, QH)
                    dve.wait_ge(S["pv_filled"], u + 1)
                    if u:
                        dve.wait_ge(S["attn_ready"], u)
                    o = banks[2 + u % 2][:, 0:4 * (DH + 1)].rearrange("p (q d) -> p q d", q=4)
                    chain.then(V.reciprocal(rden[:, :], o[:, :, DH]))
                    V.tensor_tensor(attn[:, 4 * qh:4 * qh + 4, h * DH:(h + 1) * DH], o[:, :, 0:DH],
                                    rden[:, :].unsqueeze(2).broadcast_to([P, 4, DH]), ALU.mult).then_inc(S["attn_ready"], 1)
                dve.wait_ge(S["att_filled"], 16)
                V.tensor_copy(attnT[:, BANK:N], banks[1][:, :]).then_inc(S["attnT_by_dve"], 1)
                for f in range(2):
                    dve.wait_ge(S["att_filled"], 17 + f)
                    chain(V.tensor_tensor(y[:, 4 * f:4 * f + 4, :], banks[2 + f][:, :].rearrange("p (t c) -> p t c", t=4),
                                          bo_rows[:, :].unsqueeze(1).broadcast_to([P, 4, C]), ALU.add))
                chain.settle()
                normalise(chain, y, y)
                chain.then(V.tensor_tensor(x2[:, :, :], xin[:, :, :], y[:, :, :], ALU.add))
                normalise(chain, x2n, x2)
                dve.drain().then_inc(S["x2n_ready"], 1)

                for i in range(2):
                    bank = filled("xt", i)
                    V.tensor_copy(xt[:, 4 * i:4 * i + 4, :].rearrange("p t n -> p (t n)"), bank[:, :]).then_inc(S["ffn_by_D"], 1)
                V.tensor_copy(lg[:, :], filled("logits")[:, 0:E]).then_inc(S["ffn_by_D"], 1)
                dve.wait_ge(S["ffn_by_D"], evacuated_by("D", FILL_AT["logits"]))
                top2(chain, 0)
                for k in range(2):
                    chain(V.tensor_scalar(spread[:, 0:P].rearrange("n (h k i) -> n h k i", h=2, k=2)[:, :, k],
                                          mask_half.rearrange("n (h k i) -> n h k i", h=2, k=2)[:, :, k],
                                          prob[:, k:k + 1], None, ALU.mult))
                dve.drain().then_inc(S["route_ready"], 1)
                bank = filled("route")
                V.tensor_scalar(ohA[:, :, :].rearrange("e k n -> e (k n)"), bank[:, 0:2 * P], unscale[:, 0:1], None, ALU.mult)
                V.tensor_scalar(ohB[:, :, :].rearrange("e k n -> e (k n)"), bank[:, 0:2 * P], unscale[:, 1:2], None, ALU.mult)
                V.tensor_copy(pb[:, 0:G], bank[:, 2 * P:2 * P + G]).then_inc(S["ffn_by_D"], 1)
                dve.wait_ge(S["ffn_by_D"], evacuated_by("D", FILL_AT["route"]))
                for i in range(8):
                    bank = filled("stage1", i)
                    V.tensor_tensor(tok[:, 8 * i:8 * i + 8, :], bank[:, :].rearrange("q (g p) -> q g p", g=8),
                                    pb[:, 8 * i:8 * i + 8].unsqueeze(2).broadcast_to([P, 8, F1]), ALU.mult).then_inc(S["ffn_by_D"], 1)
                for i in range(8):
                    bank = filled("stage2", i)
                    V.tensor_tensor(tok[:, 8 * i:8 * i + 8, :], bank[:, :].rearrange("q (g p) -> q g p", g=8),
                                    bup[:, :].unsqueeze(1).broadcast_to([P, 8, F1]), ALU.add).then_inc(S["ffn_by_D"], 1)
                for i in range(2):
                    bank = filled("dlogits", i)
                    V.tensor_copy(lg[G * i:G * i + G, :], bank[G * i:G * i + G, 0:E]).then_inc(S["ffn_by_D"], 1)
                dve.wait_ge(S["ffn_by_D"], evacuated_by("D", FILL_AT["dlogits"] + 1))
                top2(chain, 1)
                for k in range(2):
                    chain(V.tensor_scalar(spread[:, k * G:(k + 1) * G], mask_g, prob[:, k:k + 1], None, ALU.mult))
                dve.drain().then_inc(S["route_ready"], 1)
                bank = filled("droute")
                V.tensor_scalar(ohA[:, :, :].rearrange("e k n -> e (k n)"), bank[:, 0:2 * P], unscale[:, 2:3], None, ALU.mult)
                V.tensor_scalar(ohB[:, :, :].rearrange("e k n -> e (k n)"), bank[:, 0:2 * P], unscale[:, 3:4], None, ALU.mult)
                V.tensor_copy(pb[:, :], bank[:, 2 * P:3 * P]).then_inc(S["ffn_by_D"], 1)
                dve.wait_ge(S["ffn_by_D"], evacuated_by("D", FILL_AT["droute"]))
                for i in range(8):
                    bank = filled("dstage1", i)
                    V.tensor_tensor(tok[:, 8 * i:8 * i + 8, :].rearrange("q g (k o) -> q g k o", k=2),
                                    bank[:, :].rearrange("q (g k o) -> q g k o", g=8, k=2),
                                    pb[:, :].rearrange("q (k g) -> q g k", k=2)[:, 8 * i:8 * i + 8].unsqueeze(3).broadcast_to([P, 8, 2, D1]),
                                    ALU.mult).then_inc(S["ffn_by_D"], 1)
                dve.wait_ge(S["y_loaded"], 16)
                chain.then(V.tensor_tensor(ydn[:, :, :], ydn[:, :, :], bdn[:, :].rearrange("p (t c) -> p t c", t=T), ALU.add))
                normalise(chain, ydn, ydn)
                V.tensor_tensor(res[:, :, :], x2[:, :, :], ydn[:, :, :], ALU.add).then_inc(S["out_ready"], 1)
                dve.drain().then_inc(s_done, 1)
                dve.wait_ge(s_go["dve"], 1)
                dve.sem_clear(s_go["dve"])

        @block.tensor
        def _(pe):
            pe.wait_ge(s_const, 160)
            pe.wait_ge(s_setup, 1)
            M = nc.tensor.matmul

            def begin(stage, i=0):
                fill = FILL_AT[stage] + i
                if fill >= 4:
                    fill_wait(pe, fill - 4)
                return banks[4 + fill % 4]

            with pe.Fori(0, B) as b:
                pe.wait_ge(S["xnorm_ready"], 1)
                for t in range(T):
                    i = nc.tensor.transpose(banks[t // 4][:, P * (t % 4):P * (t % 4) + P], xn[:, t, :], ident)
                    if t % 4 == 3:
                        i.then_inc(S["att_filled"], 1)
                pe.wait_ge(S["xnT_by_act"], 1)
                pe.wait_ge(S["xnT_by_dve"], 1)
                for t in range(T):
                    if t >= 4:
                        pe.wait_ge(S["qkv_by_act"] if t % 2 == 0 else S["qkv_by_dve"], (t - 4) // 2 + 1)
                    M(banks[(2 + t) % 4][:, 0:3 * C], xnT[:, t * P:(t + 1) * P], wqkv[:, :], start=True, stop=True).then_inc(S["att_filled"], 1)
                pe.wait_ge(S["qk_scaled"], 1)
                for f in range(4):
                    for t in range(4):
                        i = nc.tensor.transpose(banks[f][:, P * t:P * t + P], qk[:, 4 * (f % 2) + t, C * (f // 2):C * (f // 2) + C], ident)
                    i.then_inc(S["att_filled"], 1)
                pe.wait_ge(S["qkT_by_act"], 2)
                pe.wait_ge(S["qkT_by_dve"], 2)

                def scores(u, kt):
                    h, qh = divmod(u, QH)
                    f = u * T + kt
                    if f >= 2:
                        pe.wait_ge(S["probs_ready"], f - 1)
                    M(banks[kt % 2][:, :], kT[h * DH:(h + 1) * DH, kt * P:(kt + 1) * P],
                      qT[h * DH:(h + 1) * DH, qh * BANK:(qh + 1) * BANK], start=True, stop=True).then_inc(S["scores_filled"], 1)

                def values(u, step):
                    h, qt, first = u // QH, step // 2, step % 2 == 0
                    if step == 0:
                        pe.wait_ge(S["probs_ready"], (u + 1) * T)
                        if u >= 2:
                            pe.wait_ge(S["attn_ready"], u - 1)
                    for kt in range(0 if first else 4, 4 if first else T):
                        i = M(banks[2 + u % 2][:, qt * (DH + 1):(qt + 1) * (DH + 1)], pT[:, u % 2, kt, qt * P:(qt + 1) * P],
                              vv[:, kt, h, :], start=(kt == 0), stop=(kt == T - 1))
                    if step == T - 1:
                        i.then_inc(S["pv_filled"], 1)

                for u in range(UNITS + 1):
                    for step in range(T):
                        if u < UNITS:
                            scores(u, step)
                        if u >= 1:
                            values(u - 1, step)
                pe.wait_ge(S["attn_ready"], UNITS)
                for t in range(T):
                    i = nc.tensor.transpose(banks[t // 4][:, P * (t % 4):P * (t % 4) + P], attn[:, t, :], ident)
                    if t % 4 == 3:
                        i.then_inc(S["att_filled"], 1)
                pe.wait_ge(S["attnT_by_act"], 1)
                pe.wait_ge(S["attnT_by_dve"], 1)
                for t in range(T):
                    i = M(banks[2 + t // 4][:, P * (t % 4):P * (t % 4) + P], attnT[:, t * P:(t + 1) * P], wo[:, :], start=True, stop=True)
                    if t % 4 == 3:
                        i.then_inc(S["att_filled"], 1)

                pe.wait_ge(S["x2n_ready"], 1)
                for f in range(2):
                    bank = begin("xt", f)
                    for t in range(4):
                        i = nc.tensor.transpose(bank[:, P * t:P * t + P], x2n[:, 4 * f + t, :], ident)
                    i.then_inc(S["ffn_filled"], 1)
                fill_wait(pe, FILL_AT["xt"] + 1)
                bank = begin("logits")
                for t in range(T):
                    i = M(bank[:, 0:E], xt[:, t, :], wup[:, t, :], start=(t == 0), stop=(t == T - 1))
                i.then_inc(S["ffn_filled"], 1)

                def route(stage, layer):
                    pe.wait_ge(S["route_ready"], layer + 1)
                    bank = begin(stage)
                    for k in range(2):
                        nc.tensor.transpose(bank[:, k * P:(k + 1) * P], oh[:, k, :], ident)
                    if layer == 0:
                        i = M(bank[:, 2 * P:2 * P + G], spread[:, 0:P], mask_g, start=True, stop=True)
                    else:
                        i = M(bank[:, 2 * P:3 * P], mask_half, spread[:, 0:P], start=True, stop=True)
                    i.then_inc(S["ffn_filled"], 1)
                    fill_wait(pe, FILL_AT[stage])

                def gather_up(stage, i, table, hot):
                    bank = begin(stage, i)
                    for e in range(8):
                        for c in range(4):
                            last = M(bank[32 * c:32 * c + 32, e * G:(e + 1) * G], table[:, (8 * i + e) * D1:(8 * i + e + 1) * D1],
                                     hot[:, c % 2, G * (c // 2):G * (c // 2) + G], start=True, stop=True)
                    last.then_inc(S["ffn_filled"], 1)

                def gather_down(stage, i, table, hot):
                    bank = begin(stage, i)
                    for e in range(4):
                        for h in range(2):
                            last = M(bank[G * h:G * h + G, e * P:(e + 1) * P], table[:, (4 * i + e) * F1:(4 * i + e + 1) * F1],
                                     hot[:, :, G * h:G * h + G], start=True, stop=True)
                    last.then_inc(S["ffn_filled"], 1)

                def per_token(stage, left, right):
                    open_banks = {}
                    for s in range(9):
                        if s < 8:
                            open_banks[s] = begin(stage, s)
                            for g in range(8 * s, 8 * s + 8):
                                M(open_banks[s][0:G, (g % 8) * F1:(g % 8 + 1) * F1], left[0:G, g, :], right[0:G, g, :], start=True, stop=True)
                        if s >= 1:
                            for g in range(8 * s - 8, 8 * s):
                                last = M(open_banks[s - 1][G:P, (g % 8) * F1:(g % 8 + 1) * F1], left[G:P, g, :], right[G:P, g, :],
                                         start=True, stop=True)
                            last.then_inc(S["ffn_filled"], 1)

                route("route", 0)
                for i in range(8):
                    gather_up("gather_b", i, tab[1], ohB)
                fill_wait(pe, FILL_AT["gather_b"] + 7)
                pe.wait_ge(S["xbd_ready"], 1)
                for i in range(8):
                    bank = begin("stage1", i)
                    for g in range(8 * i, 8 * i + 8):
                        last = M(bank[:, (g % 8) * F1:(g % 8 + 1) * F1], xbd[:, g, :], gb[:, g, :], start=True, stop=True)
                    last.then_inc(S["ffn_filled"], 1)
                for i in range(8):
                    gather_up("gather_a", i, tab[0], ohA)
                fill_wait(pe, FILL_AT["gather_a"] + 7)
                per_token("stage2", ga, tok)
                pe.wait_ge(S["hidden_ready"], 8)
                for h in range(2):
                    bank = begin("dlogits", h)
                    for p in range(F1):
                        last = M(bank[G * h:G * h + G, 0:E], tok[G * h:G * h + G, :, p], wdn[G * h:G * h + G, p, :],
                                 start=(p == 0), stop=(p == F1 - 1))
                    last.then_inc(S["ffn_filled"], 1)
                route("droute", 1)
                for i in range(8):
                    gather_down("dgather_a", i, tab[2], ohA)
                for i in range(8):
                    gather_down("dgather_b", i, tab[3], ohB)
                fill_wait(pe, FILL_AT["dgather_b"] + 7)
                per_token("dstage1", tok, gb)
                fill_wait(pe, FILL_AT["dstage1"] + 7)
                for h in range(2):
                    bank = begin("dstage2", h)
                    for g in range(G):
                        for k in range(2):
                            last = M(bank[32 * (g % 4):32 * (g % 4) + 32, (g // 4) * D1:(g // 4 + 1) * D1],
                                     tok[G * h:G * h + G, g, k * D1:(k + 1) * D1], ga[G * h:G * h + G, g, k * D1:(k + 1) * D1],
                                     start=(k == 0), stop=(k == 1))
                    last.then_inc(S["ffn_filled"], 1)
                pe.drain().then_inc(s_done, 1)
                pe.wait_ge(s_go["pe"], 1)
                pe.sem_clear(s_go["pe"])


def kernel(L0_attn_x, L0_attn_Wq, L0_attn_Wk, L0_attn_Wv, L0_attn_Wo, L0_attn_bo, L0_attn_ln_g, L0_attn_ln_b,
           L0_attn_q_gamma, L0_attn_k_gamma, L0_ffn_W_up, L0_ffn_A_up, L0_ffn_B_up, L0_ffn_scale_up, L0_ffn_bias_up,
           L0_ffn_W_down, L0_ffn_A_down, L0_ffn_B_down, L0_ffn_scale_down, L0_ffn_bias_down):
    import concourse.bacc as bacc
    from concourse.bass_utils import run_bass_kernel_spmd

    a = {k: np.asarray(v) for k, v in locals().items() if k.startswith("L0_")}

    def rows(v):
        return np.ascontiguousarray(np.broadcast_to(v.reshape(1, -1), (P, v.size)))

    n = np.arange(P)
    shape_consts = np.concatenate([
        np.eye(P), np.broadcast_to(n % E, (P, P)), (n[:, None] // G == n[None, :] // G),
        (n[:, None] % G == np.arange(G)[None, :]), -(n[:, None] >= E).astype(float)], axis=1).astype(np.float32)
    w_down = a["L0_ffn_W_down"].reshape(E, F1, F1).transpose(1, 2, 0)
    bias_up = a["L0_ffn_bias_up"].reshape(F1, F1)
    ins = {
        "x": a["L0_attn_x"],
        "w_qkv": np.concatenate([a["L0_attn_Wq"].T, a["L0_attn_Wk"].T, a["L0_attn_Wv"].T], axis=1),
        "w_o": a["L0_attn_Wo"].T,
        "bo": rows(a["L0_attn_bo"]),
        "ln_gamma": np.stack([a["L0_attn_ln_g"], a["L0_attn_ln_b"], np.tile(a["L0_attn_q_gamma"], HEADS),
                              np.tile(a["L0_attn_k_gamma"], HEADS)], axis=1),
        "a_up": a["L0_ffn_A_up"].reshape(E, -1),
        "b_up": a["L0_ffn_B_up"].reshape(E, -1),
        "a_down": a["L0_ffn_A_down"].reshape(E, -1),
        "b_down": a["L0_ffn_B_down"].reshape(E, -1),
        "w_up": a["L0_ffn_W_up"].reshape(E, T, C).transpose(2, 1, 0),
        "w_down": np.concatenate([w_down, w_down], axis=0),
        "bias_up": np.concatenate([bias_up, bias_up], axis=0),
        "bias_down": rows(a["L0_ffn_bias_down"]),
        "scales": np.concatenate([rows(a["L0_ffn_scale_up"]), rows(a["L0_ffn_scale_down"])], axis=1),
        "shape_consts": shape_consts,
    }
    ins = {k: np.ascontiguousarray(v) for k, v in ins.items()}
    nc = bacc.Bacc("TRN2", target_bir_lowering=False, num_devices=1)
    h = {k: nc.dram_tensor(f"in_{k}", v.shape, mybir.dt.from_np(v.dtype), kind="ExternalInput").ap() for k, v in ins.items()}
    out = nc.dram_tensor("out", (B, N, C), F32, kind="ExternalOutput").ap()
    tables = [h.pop(k) for k in ("a_up", "b_up", "a_down", "b_down")]
    build_program(nc, tables=tables, out=out, **h)
    r = run_bass_kernel_spmd(nc, [{f"in_{k}": v for k, v in ins.items()}], core_ids=[0])
    return r.results[0]["out"]
```

```python
from contextlib import ExitStack

import numpy as np

import concourse.bass as bass
from concourse import mybir

ALU = mybir.AluOpType
ACT = mybir.ActivationFunctionType
AX = mybir.AxisListType
F32 = mybir.dt.float32
F16 = mybir.dt.float16
BF16 = mybir.dt.bfloat16
I32 = mybir.dt.int32
U32 = mybir.dt.uint32

P = 128
B, N, C = 8, 1024, 128
HEADS, DH = 2, 64
ONES = 32
OROWS = DH + ONES
T = N // P
E = 64
D1, F1 = 32, 64
G = P // 2
BANK = 512
QH = N // BANK
UNITS = HEADS * QH
EPS = 1e-5
RMS_FLOOR = 1e-16
EXP_TOP = 80.0


class Count:

    def __init__(self, eng, sem):
        self.eng, self.sem, self.n = eng, sem, 0

    def __call__(self, instruction):
        self.n += 1
        return instruction.then_inc(self.sem, 1)

    def settle(self):
        self.eng.wait_ge(self.sem, self.n)

    def then(self, instruction):
        self(instruction)
        self.settle()


FFN_FILLS = [
    ("xt", 2, "DD"), ("logits", 1, "D"), ("route", 1, "D"),
    ("gather_b", 8, "ADADADAD"), ("stage1", 8, "DDDDDDDD"), ("gather_a", 8, "ADADADAD"), ("stage2", 8, "DDDDDDDD"),
    ("dlogits", 2, "DD"), ("droute", 1, "D"),
    ("dgather_a", 8, "AAAAAAAA"), ("dgather_b", 8, "AAAAAAAA"), ("dstage1", 8, "DDDDDDDD"), ("dstage2", 2, "AA"),
]
FILL_AT, FILL_BY = {}, []
for _name, _n, _by in FFN_FILLS:
    FILL_AT[_name] = len(FILL_BY)
    FILL_BY += list(_by)


def evacuated_by(engine, fill):
    return FILL_BY[:fill + 1].count(engine)


def s_(*n):
    return [("scores", i) for i in n]


def v_(*n):
    return [("values", i) for i in n]


def interleave(stage, count, between):
    steps = []
    for i in range(count):
        steps += [(stage, i)] + (between[i] if i < len(between) else [])
    return steps


STEADY = s_(0, 1) + [("xt", 0), ("xt", 1)] + s_(2, 3) + [("logits", 0), ("top2", 0)] + s_(4, 5, 6) + v_(0, 1) + [("route", 0)] + v_(2, 3)
STEADY += interleave("gather_b", 8, [[("xbd", i)] + f for i, f in enumerate(
    [s_(7), v_(4), s_(8), v_(5), s_(9), v_(6), s_(10), v_(7)])])
STEADY += s_(11) + v_(8)
STEADY += interleave("stage1", 8, [[], [("end", 0)], [], [("end", 1)], [("end", 2)], [("end", 3), ("seed", 0)], [], []])
STEADY += interleave("gather_a", 8, [s_(12), v_(9), s_(13), v_(10), s_(14), v_(11), s_(15), v_(12)])
STEADY += s_(16) + v_(13)
STEADY += interleave("stage2", 9, [s_(17), v_(14) + [("norm1", 0)], s_(18), s_(19) + [("norm1", 1)], s_(20), s_(21) + [("norm1", 2)], s_(22), s_(23)])
STEADY += [("gelu", i) for i in range(8)] + v_(*range(15, 22)) + s_(24, 25)
STEADY += interleave("dlogits", 8, [s_(26), v_(22), s_(27), v_(23), s_(28), v_(24), s_(29)])
STEADY += [("top2", 1)] + s_(30, 31) + v_(25, 26) + [("droute", 0)] + v_(27, 28)
STEADY += interleave("dgather_a", 8, [v_(29), v_(30), v_(31), [("xnT", 0)], [("xnT", 1)]])
STEADY += interleave("dgather_b", 8, [[("wo", i)] for i in range(8)])
STEADY += [("qkv", 0)]
STEADY += interleave("dstage1", 9, [[("qkv", 1)], [("qkv", 2), ("norm_y", 0)], [("qkv", 3), ("norm_y", 1)], [("qkv", 4), ("norm_y", 2)],
                                    [("qkv", 5)], [("qkv", 6), ("norm_y", 3)], [("qkv", 7)], [], [("rms", 0)]])
STEADY += [("qkT", 0), ("qkT", 1), ("norm2", 0), ("norm2", 1), ("norm2", 2)]
STEADY += interleave("dstage2", 8, [[], [], [], [], [("qkT", 2)], [], [("qkT", 3)]])
FRONT = {"norm1", "xnT", "qkv", "rms", "qkT"}
BACK = {"scores", "values", "wo", "norm_y", "norm2"}
START = [s for s in STEADY if s[0] in FRONT]
PROLOGUE = []
for _s in STEADY:
    PROLOGUE += [_s] if _s[0] in FRONT | BACK | {"seed"} else []
    PROLOGUE += [("tables", (1, 5, 9, 13).index(_s[1]))] if _s[0] == "values" and _s[1] in (1, 5, 9, 13) else []
FIRST = [s for s in STEADY if s[0] != "end"]
SHORT = [s for s in STEADY if s[0] not in FRONT]
LAST = [s for s in STEADY if s[0] not in FRONT | BACK]
END = [("end", i) for i in range(4)]
ATT_FILLS = {"xnT", "wo", "qkv", "qkT"}


NORMS = {"norm1", "norm_y", "norm2", "end"}
NORM_SLOT = {"norm1": 0, "norm_y": 1, "norm2": 2, "end": 3}


def norm_count(steps, step):
    return [s[0] for s in steps if s[0] in NORMS and s[1] == 2].index(step) + 1


def att_fill(steps, step, i):
    return [s for s in steps if s[0] in ATT_FILLS].index((step, i)) + 1


def build_program(nc, x, w_qkv, w_o, bo, ln_gamma, tables, w_up, w_down, bias_up, bias_down, scales, shape_consts, out):
    with ExitStack() as ctx:
        def sb(name, shape, dt=F32):
            return ctx.enter_context(nc.sbuf_tensor(name, shape, dt))

        wqkv = sb("wqkv", [P, 3 * C])
        wo = sb("wo", [OROWS, HEADS, C + 1])
        bo_rows = sb("bo_rows", [P, C])
        gam = sb("gam", [P, 4])
        wup = sb("wup", [P, T, E])
        wdn = sb("wdn", [P, F1, E])
        bup = sb("bup", [P, F1])
        bdn = sb("bdn", [P, N])
        scl = sb("scl", [P, 2])
        tab = [sb(f"tab{i}", [P, 2048], F16) for i in range(4)]
        unscale = sb("unscale", [P, 4])
        cst = sb("cst", [P, 3 * P + G + 1])
        ident, iota = cst[:, 0:P], cst[:, P:2 * P]
        mask_half, mask_g = cst[:, 2 * P:3 * P], cst[:, 3 * P:3 * P + G]
        mask_low = cst[:, 3 * P + G:3 * P + G + 1]
        shift = sb("shift", [P, 2])

        xin = sb("xin", [P, T, C])
        xn = sb("xn", [P, T, C])
        xnT = sb("xnT", [P, T * P])
        qk = sb("qk", [P, T, 2 * C])
        vv = sb("vv", [P, T, HEADS, OROWS])
        vv_flat = vv[:, :, :, :].rearrange("p t h d -> p t (h d)")
        qT = sb("qT", [P, N])
        kT = sb("kT", [P, N])
        pT = sb("pT", [P, 2, T, BANK])
        y = pT[:, 0, 0:2, :].rearrange("p a b -> p (a b)").rearrange("p (t c) -> p t c", t=T)
        sq = pT[:, 1, 0:4, :].rearrange("p a b -> p (a b)").rearrange("p (t c) -> p t c", t=T)
        oT = qk[:, :, :].rearrange("p a b -> p (a b)").rearrange("p (u n) -> p u n", u=UNITS)

        x2 = sb("x2", [P, T, C])
        x2n = sb("x2n", [P, T, C])
        x2_old = sb("x2_old", [P, T, C])
        ydn = x2n
        xt = sb("xt", [P, T, P])
        ys = xn[:, :, :].rearrange("p a b -> p (a b)")
        xbd = sb("xbd", [P, G, P])
        stage = xbd[:, :, :].rearrange("p a b -> p (a b)").rearrange("p (i n) -> p i n", i=4)
        gb = sb("gb", [P, G, F1])
        ga = sb("ga", [P, G, F1])
        tok = sb("tok", [P, G, F1])
        lg = ga[:, 6, :]
        m8, i8, idx, gap, prob = ga[:, 7, 0:8], ga[:, 7, 8:16].bitcast(U32), ga[:, 7, 16:18], ga[:, 7, 18:22], ga[:, 7, 22:24]
        oh = ga[:, 0:4, :].rearrange("p a b -> p (a b)").rearrange("p (k n) -> p k n", k=2)
        spread = ga[:, 4:6, :].rearrange("p a b -> p (a b)")
        ohA = sb("ohA", [P, 2, P], BF16)
        ohB = sb("ohB", [P, 2, P], BF16)
        pb = sb("pb", [P, P])

        bn = sb("bn", [P, T, 6])
        mv = sb("mv", [P, T, 2])
        factor = sb("factor", [P, len(NORMS), 2, T])
        k_scale = sb("k_scale", [P, T, HEADS])
        ssq = sb("ssq", [P, 4 * T])
        rs = sb("rs", [P, 4 * T])
        rt = sb("rt", [P, 4 * T])
        rv = sb("rv", [P, 4 * T])
        rden = sb("rden", [P, T, HEADS])
        ms, bits = ga[:, 0, 0:4], ga[:, 0, 4:6].bitcast(I32)

        banks = [ctx.enter_context(nc.psum_tensor(f"bank{i}", [P, BANK], F32)) for i in range(8)]

        def sem(name):
            return ctx.enter_context(nc.semaphore(name))

        s_attw, s_ffnw = sem("attention_weights_loaded"), sem("ffn_weights_loaded")
        s_tab = [sem(f"table{i}_loaded") for i in range(4)]
        s_setup, s_tabs, s_setchain = sem("setup_done"), sem("tables_split"), sem("setup_chain")
        s_bound, s_bound_all = sem("bound_ready"), sem("bound_spread")
        s_done, s_go = sem("engines_done"), {k: sem(f"go_{k}") for k in ("sp", "act", "pe", "dve")}
        names = ["x_loaded", "norm_ready", "norm_applied", "att_filled", "xnT_by_act", "xnT_by_dve", "qkv_ready", "squares_ready",
                 "qk_scaled", "qkT_by_act", "qkT_by_dve", "scores_filled", "probs_ready", "pv_filled", "oT_by_act", "oT_by_dve",
                 "y_rows", "ffn_filled", "ffn_by_A", "ffn_by_D", "xbd_by_act", "xbd_by_dve", "xbd_by_pool", "gap_ready", "gap_exp",
                 "hidden_ready", "route_ready", "ys_stored", "y_loaded", "out_ready", "out_stored", "x2_kept", "x2_seeded", "dve_chain"]
        S = {n: sem(n) for n in names}
        nums = sorted(S[n].num for n in names)
        assert nums == list(range(nums[0], nums[0] + len(names)))

        scratch = nc.dram_tensor("y_scratch", [P, N], F32).ap()
        x_v = x.rearrange("b (p t) c -> (b p) t c", t=T)
        out_v = out.rearrange("b (p t) c -> (b p) t c", t=T)

        block = ctx.enter_context(nc.Block())

        def normed(step):
            return {"norm1": (xn, xin), "norm_y": (y, y), "norm2": (x2n, x2), "end": (ydn, ydn)}[step]

        def x_block(n):
            cb, c = divmod(n, 4)
            return (xbd[32 * c:32 * c + 32, :, 32 * c + cb:32 * c + 32:4].rearrange("j g t -> j t g"),
                    xt[32 * cb:32 * cb + 32, :, G * (c // 2):G * (c // 2) + G])

        def evacuate_gather(eng, who, copy, stage, i, dst):
            fill = FILL_AT[stage] + i
            eng.wait_ge(S["ffn_filled"], fill + 1)
            bank = banks[4 + fill % 4]
            if stage[0] == "d":
                src = bank[:, :].rearrange("q (e k g) -> q e k g", e=4, k=2)
                to = dst[:, :, :].rearrange("q g (k e) -> q e k g", k=2)[:, 4 * i:4 * i + 4]
                for k in range(2):
                    last = copy(to[:, :, k], src[:, :, k])
            else:
                last = copy(dst[:, :, :].rearrange("q g e -> q e g")[:, 8 * i:8 * i + 8], bank[:, :].rearrange("q (e g) -> q e g", e=8))
            last.then_inc(S[f"ffn_by_{who}"], 1)

        def iterations(eng, run):
            run(-2, START)
            run(-1, PROLOGUE)
            run(0, FIRST)
            with eng.Fori(1, B - 2) as b:
                run(b, STEADY)
            run(B - 2, SHORT)
            run(B - 1, LAST)
            run(B, END)

        def meet(eng, name):
            eng.drain().then_inc(s_done, 1)
            eng.wait_ge(s_go[name], 1)
            eng.sem_clear(s_go[name])

        @block.sync
        def _(sp):
            def load_x(b):
                sp.dma_start(xin[:, :, :], x_v[bass.ds(b * P, P)]).then_inc(S["x_loaded"], 16)

            def run(b, steps):
                if steps is START:
                    load_x(0)
                    for dst, src in [(cst[:, :], shape_consts), (gam[:, :], ln_gamma), (wqkv[:, :], w_qkv), (wo[:, :, :], w_o),
                                     (bo_rows[:, :], bo)]:
                        sp.dma_start(dst, src).then_inc(s_attw, 16)
                    for i in range(4):
                        for half in range(2):
                            sp.dma_start(stage[half * E:(half + 1) * E, i, :], tables[i]).then_inc(s_tab[i], 16)
                    for dst, src in [(wup[:, :, :], w_up), (wdn[:, :, :], w_down), (bup[:, :], bias_up), (bdn[:, :], bias_down),
                                     (scl[:, :], scales)]:
                        sp.dma_start(dst, src).then_inc(s_ffnw, 16)
                    sp.wait_ge(s_ffnw, 80)
                if ("end", 0) in steps:
                    for c in range(4):
                        sp.dma_start(scratch.rearrange("(s c) (o p) -> c o s p", c=4, p=D1)[c],
                                     ys[c * D1:(c + 1) * D1, :].rearrange("o (s p) -> o s p", p=D1)).then_inc(S["ys_stored"], 16)
                    sp.wait_ge(S["ys_stored"], 64)
                    if ("xt", 0) in steps:
                        sp.wait_ge(S["ffn_filled"], FILL_AT["xt"] + 2)
                    sp.dma_start(ydn[:, :, :], scratch.rearrange("n (t c) -> n t c", t=T)).then_inc(S["y_loaded"], 16)
                    sp.wait_ge(S["out_ready"], 1)
                    sp.dma_start(out_v[bass.ds((b - 1) * P, P)], ydn[:, :, :]).then_inc(S["out_stored"], 16)
                if ("norm1", 0) in steps and steps is not START:
                    sp.wait_ge(S["x2_seeded"], 1)
                    load_x(b + 2)
                if ("end", 0) in steps:
                    sp.wait_ge(S["out_stored"], 16)
                meet(sp, "sp")

            iterations(sp, run)

        @block.gpsimd
        def _(pool):
            def run(b, steps):
                if steps is START:
                    pool.wait_ge(s_bound, 1)
                    nc.gpsimd.partition_all_reduce(shift[:, 1:2], shift[:, 0:1], P, bass.bass_isa.ReduceOp.max).then_inc(s_bound_all, 1)
                for step, i in steps:
                    if step == "xbd" and i % 2 == 1:
                        pool.wait_ge(S["ffn_by_D"], 2)
                        if i > 1:
                            pool.wait_ge(S["xbd_by_pool"], i // 2)
                        dst, src = x_block(2 * i + 1)
                        nc.gpsimd.tensor_scalar(dst, src, 1.0, None, ALU.mult).then_inc(S["xbd_by_pool"], 1)
                pool.drain()
                pool.wait_ge(s_done, 4)
                pool.sem_clear(range(nums[0], nums[0] + len(names)))
                pool.sem_clear(s_done)
                for k in ("sp", "act", "pe", "dve"):
                    pool.sem_inc(s_go[k], 1)

            iterations(pool, run)

        @block.scalar
        def _(act):
            A = nc.scalar
            act.wait_ge(s_attw, 80)

            def copy(dst, src):
                return A.activation(dst, src, ACT.Copy)

            def run(b, steps):
                for step, i in steps:
                    if step == "xnT" and i == 0:
                        act.wait_ge(S["att_filled"], att_fill(steps, step, i))
                        A.activation(xnT[:, 0:BANK], banks[0][:, :], ACT.Identity, bias=gam[:, 1:2], scale=gam[:, 0:1])\
                            .then_inc(S["xnT_by_act"], 1)
                    elif step == "qkv":
                        act.wait_ge(S["att_filled"], att_fill(steps, step, i))
                        bank = banks[(2 + i) % 4]
                        A.activation(sq[:, i, :], bank[:, 0:2 * C], ACT.Square).then_inc(S["squares_ready"], 1)
                        copy(qk[:, i, :], bank[:, 0:2 * C])
                        copy(vv[:, i, :, 0:DH], bank[:, 2 * C:3 * C].rearrange("p (h d) -> p h d", h=HEADS)).then_inc(S["qkv_ready"], 1)
                    elif step == "qkT" and i % 2 == 0:
                        act.wait_ge(S["att_filled"], att_fill(steps, step, i))
                        dst, col = ((kT, 3), (qT, 2))[i // 2]
                        A.activation(dst[:, 0:BANK], banks[(2 + i) % 4][:, :], ACT.Copy, scale=gam[:, col:col + 1]).then_inc(S["qkT_by_act"], 1)
                    elif step == "scores":
                        u, kt = divmod(i, T)
                        if steps is PROLOGUE and i == 0:
                            act.wait_ge(s_setup, 1)
                        if u >= 2:
                            act.wait_ge(S["pv_filled"], i + 1 - 2 * T)
                        act.wait_ge(S["scores_filled"], i + 1)
                        A.activation(pT[:, u % 2, kt, :], banks[kt % 2][:, :], ACT.Exp, bias=shift[:, 0:1],
                                     scale=k_scale[:, kt, u // QH:u // QH + 1]).then_inc(S["probs_ready"], 1)
                    elif step == "values" and i % (2 * T) == T - 1:
                        u = i // T
                        act.wait_ge(S["pv_filled"], i + 1)
                        copy(oT[0:OROWS, u, :], banks[2 + u % 2][0:OROWS, :]).then_inc(S["oT_by_act"], 1)
                    elif step == "top2":
                        act.wait_ge(S["gap_ready"], i + 1)
                        A.activation(gap[:, 1:2], gap[:, 0:1], ACT.Exp).then_inc(S["gap_exp"], 1)
                    elif step in NORMS and i == 2:
                        dst, src = normed(step)
                        act.wait_ge(S["norm_ready"], norm_count(steps, step))
                        if step == "norm1" and ("end", 0) in steps:
                            act.wait_ge(S["ys_stored"], 64)
                        if step == "norm2" and ("end", 0) in steps:
                            act.wait_ge(S["out_stored"], 16)
                        for t in range(T):
                            last = A.activation(dst[:, t, :], src[:, t, :], ACT.Identity, scale=factor[:, NORM_SLOT[step], 0, t:t + 1],
                                                bias=factor[:, NORM_SLOT[step], 1, t:t + 1])
                        last.then_inc(S["norm_applied"], 1)
                    elif step == "seed":
                        if ("xt", 0) in steps:
                            if ("end", 0) in steps:
                                act.wait_ge(S["out_ready"], 1)
                            copy(x2_old[:, :, :], x2[:, :, :]).then_inc(S["x2_kept"], 1)
                        if ("wo", 0) in steps:
                            if ("xt", 0) in steps:
                                act.wait_ge(S["x2_kept"], 1)
                            copy(x2[:, :, :], xin[:, :, :]).then_inc(S["x2_seeded"], 1)
                    elif step == "xbd":
                        act.wait_ge(S["ffn_by_D"], 2)
                        copy(*x_block(2 * i)).then_inc(S["xbd_by_act"], 1)
                    elif step in ("gather_b", "gather_a", "dgather_a", "dgather_b") and FILL_BY[FILL_AT[step] + i] == "A":
                        evacuate_gather(act, "A", copy, step, i, gb if step in ("gather_b", "dgather_a") else ga)
                    elif step == "gelu":
                        act.wait_ge(S["ffn_by_D"], evacuated_by("D", FILL_AT["stage2"] + i))
                        A.activation(tok[:, 8 * i:8 * i + 8, :], tok[:, 8 * i:8 * i + 8, :], ACT.Gelu).then_inc(S["hidden_ready"], 1)
                    elif step == "dstage2" and i == 7:
                        for h in range(2):
                            fill = FILL_AT["dstage2"] + h
                            act.wait_ge(S["ffn_filled"], fill + 1)
                            A.activation(ys[:, BANK * h:BANK * h + BANK], banks[4 + fill % 4][:, :], ACT.Copy).then_inc(S["ffn_by_A"], 1)
                meet(act, "act")

            iterations(act, run)

        @block.vector
        def _(dve):
            V = nc.vector
            setup = Count(dve, s_setchain)
            dve.wait_ge(s_attw, 80)
            setup(V.memset(vv[:, :, :, DH:OROWS], 1.0))
            setup.then(V.tensor_tensor(ms[:, 0:1], gam[:, 2:3], gam[:, 3:4], ALU.mult))
            setup.then(V.tensor_scalar(ms[:, 1:2], ms[:, 0:1], -1.0, None, ALU.mult))
            V.tensor_tensor(shift[:, 0:1], ms[:, 0:1], ms[:, 1:2], ALU.max).then_inc(s_bound, 1)
            dve.wait_ge(s_bound_all, 1)
            setup.then(V.tensor_scalar(ms[:, 2:3], shift[:, 1:2], -(DH ** 0.5), EXP_TOP, ALU.mult, ALU.add))
            V.tensor_scalar(shift[:, 0:1], ms[:, 2:3], 0.0, None, ALU.min).then_inc(s_setup, 1)
            dve.wait_ge(s_setup, 1)

            def split_table(i):
                dve.wait_ge(s_tab[i], 32)
                setup(V.tensor_reduce(ms[:, 0:1], stage[:, i, :], AX.X, ALU.max))
                setup.then(V.tensor_reduce(ms[:, 1:2], stage[:, i, :], AX.X, ALU.min))
                setup.then(V.scalar_tensor_tensor(out=ms[:, 2:3], in0=ms[:, 1:2], scalar=-1.0, in1=ms[:, 0:1], op0=ALU.mult, op1=ALU.max))
                setup.then(V.tensor_scalar(ms[:, 3:4], ms[:, 2:3], 1e-30, None, ALU.max))
                setup.then(V.tensor_scalar(bits[:, 0:1], ms[:, 3:4].bitcast(I32), 0x7F800000, None, ALU.bitwise_and))
                setup.then(V.tensor_scalar(unscale[:, i:i + 1], bits[:, 0:1].bitcast(F32), 2.0 ** -13, None, ALU.mult))
                setup.then(V.tensor_scalar(bits[:, 1:2], unscale[:, i:i + 1].bitcast(I32), -1, 0x7F000000, ALU.mult, ALU.add))
                setup.then(V.tensor_scalar(stage[:, i, :], stage[:, i, :], bits[:, 1:2].bitcast(F32), None, ALU.mult))
                setup.then(V.tensor_copy(tab[i][:, :], stage[:, i, :]))
                setup.then(V.scalar_tensor_tensor(out=tab[i][:, :], in0=tab[i][:, :], scalar=mask_low, in1=stage[:, i, :],
                                                  op0=ALU.mult, op1=ALU.add))
                if i == 3:
                    V.memset(xbd[:, :, :], 0.0).then_inc(s_tabs, 1)

            def rsqrt(chain, n, dst):
                chain.then(V.tensor_scalar(rs[:, 0:n].bitcast(I32), rv[:, 0:n].bitcast(I32), -0.5, float(0x5F3759DF), ALU.mult, ALU.add))
                for step in range(3):
                    chain.then(V.scalar_tensor_tensor(out=rt[:, 0:n], in0=rs[:, 0:n], scalar=-0.5, in1=rs[:, 0:n], op0=ALU.mult, op1=ALU.mult))
                    chain.then(V.tensor_tensor(rt[:, 0:n], rt[:, 0:n], rv[:, 0:n], ALU.mult))
                    chain.then(V.scalar_tensor_tensor(out=dst if step == 2 else rs[:, 0:n], in0=rt[:, 0:n], scalar=1.5, in1=rs[:, 0:n],
                                                      op0=ALU.add, op1=ALU.mult))

            def statistics(chain, src):
                for t in range(T):
                    chain(V.bn_stats(bn[:, t, :], src[:, t, :]))
                chain.settle()
                for t in range(T):
                    chain(V.bn_aggr(mv[:, t, :], bn[:, t, :]))
                chain.settle()

            def factors(chain, step):
                a, c = (1.0 + EPS, EPS * EPS) if step == "norm1" else (1.0, EPS)
                chain.then(V.tensor_scalar(rv[:, 0:T], mv[:, :, 1], a, c, ALU.mult, ALU.add))
                slot = NORM_SLOT[step]
                rsqrt(chain, T, factor[:, slot, 0, :])
                V.scalar_tensor_tensor(out=factor[:, slot, 1, :], in0=mv[:, :, 0], scalar=-1.0, in1=factor[:, slot, 0, :],
                                       op0=ALU.mult, op1=ALU.mult).then_inc(S["norm_ready"], 1)

            def top2(chain, layer):
                chain.then(V.max(m8[:, :], lg[:, :]))
                V.tensor_tensor(gap[:, 0:1], m8[:, 1:2], m8[:, 0:1], ALU.subtract).then_inc(S["gap_ready"], 1)
                chain.then(V.max_index(i8[:, :], m8[:, :], lg[:, :]))
                chain.then(V.tensor_copy(idx[:, :], i8[:, 0:2]))
                for k in range(2):
                    chain(V.tensor_scalar(oh[:, k, :], iota, idx[:, k:k + 1], None, ALU.is_equal))
                dve.wait_ge(S["gap_exp"], layer + 1)
                chain.then(V.tensor_scalar(gap[:, 2:3], gap[:, 1:2], 1.0, None, ALU.add))
                chain.then(V.reciprocal(gap[:, 3:4], gap[:, 2:3]))
                chain.then(V.tensor_tensor(prob[:, 0:1], gap[:, 3:4], scl[:, layer:layer + 1], ALU.mult))
                chain.then(V.tensor_tensor(prob[:, 1:2], gap[:, 1:2], prob[:, 0:1], ALU.mult))
                for k in range(2):
                    if layer == 0:
                        to = spread[:, 0:P].rearrange("n (h k i) -> n h k i", h=2, k=2)[:, :, k]
                        mask = mask_half.rearrange("n (h k i) -> n h k i", h=2, k=2)[:, :, k]
                    else:
                        to, mask = spread[:, k * G:(k + 1) * G], mask_g
                    chain(V.tensor_scalar(to, mask, prob[:, k:k + 1], None, ALU.mult))
                dve.drain().then_inc(S["route_ready"], 1)

            def filled(stage, i=0):
                fill = FILL_AT[stage] + i
                dve.wait_ge(S["ffn_filled"], fill + 1)
                return banks[4 + fill % 4]

            def run(b, steps):
                chain = Count(dve, S["dve_chain"])
                for step, i in steps:
                    if step == "tables":
                        split_table(i)
                    elif step in NORMS and i == 0:
                        if step == "norm1":
                            dve.wait_ge(S["x_loaded"], 16)
                        elif step == "norm_y":
                            dve.wait_ge(S["y_rows"], T)
                        elif step == "end":
                            dve.wait_ge(S["y_loaded"], 16)
                            chain.then(V.tensor_tensor(ydn[:, :, :], ydn[:, :, :], bdn[:, :].rearrange("p (t c) -> p t c", t=T), ALU.add))
                        statistics(chain, normed(step)[1])
                    elif step in NORMS and i == 1:
                        factors(chain, step)
                    elif step == "norm_y" and i == 3:
                        dve.wait_ge(S["x2_seeded"], 1)
                        dve.wait_ge(S["norm_applied"], norm_count(steps, step))
                        chain.then(V.tensor_tensor(x2[:, :, :], x2[:, :, :], y[:, :, :], ALU.add))
                    elif step == "end" and i == 3:
                        dve.wait_ge(S["norm_applied"], norm_count(steps, step))
                        V.tensor_tensor(ydn[:, :, :], x2_old[:, :, :], ydn[:, :, :], ALU.add).then_inc(S["out_ready"], 1)
                    elif step == "xnT" and i == 1:
                        dve.wait_ge(S["att_filled"], att_fill(steps, step, i))
                        V.tensor_scalar(xnT[:, BANK:N], banks[1][:, :], gam[:, 0:1], gam[:, 1:2], ALU.mult, ALU.add)\
                            .then_inc(S["xnT_by_dve"], 1)
                    elif step == "qkv":
                        dve.wait_ge(S["squares_ready"], i + 1)
                        chain(V.tensor_reduce(ssq[:, 4 * i:4 * i + 4], sq[:, i, :].rearrange("p (m d) -> p m d", d=DH), AX.X, ALU.add))
                    elif step == "rms":
                        chain.settle()
                        dve.wait_ge(S["qkv_ready"], T)
                        chain.then(V.tensor_scalar(rv[:, 0:4 * T], ssq[:, :], 1.0 / DH, RMS_FLOOR, ALU.mult, ALU.max))
                        rsqrt(chain, 4 * T, rs[:, 0:4 * T])
                        rms = rs[:, 0:4 * T].rearrange("p (t m) -> p t m", t=T)
                        for half in range(2):
                            t = slice(4 * half, 4 * half + 4)
                            q = qk[:, t, 0:C].rearrange("p t (h d) -> p t h d", h=HEADS)
                            V.tensor_tensor(q, q, rms[:, t, 0:HEADS].unsqueeze(3).broadcast_to([P, 4, HEADS, DH]), ALU.mult)\
                                .then_inc(S["qk_scaled"], 1)
                        chain.then(V.tensor_scalar(k_scale[:, :, :], rms[:, :, HEADS:2 * HEADS], DH ** -0.5, None, ALU.mult))
                    elif step == "qkT" and i % 2 == 1:
                        dve.wait_ge(S["att_filled"], att_fill(steps, step, i))
                        dst, col = ((kT, 3), (qT, 2))[i // 2]
                        V.tensor_scalar(dst[:, BANK:N], banks[(2 + i) % 4][:, :], gam[:, col:col + 1], None, ALU.mult).then_inc(S["qkT_by_dve"], 1)
                    elif step == "values" and i % (2 * T) == 2 * T - 1:
                        u = i // T
                        dve.wait_ge(S["pv_filled"], i + 1)
                        V.tensor_copy(oT[0:OROWS, u, :], banks[2 + u % 2][0:OROWS, :]).then_inc(S["oT_by_dve"], 1)
                    elif step == "wo":
                        dve.wait_ge(S["att_filled"], att_fill(steps, step, i))
                        o = banks[(2 + i) % 4][:, 0:HEADS * (C + 1)].rearrange("p (h c) -> p h c", h=HEADS)
                        chain.then(V.reciprocal(rden[:, i, :], o[:, :, C]))
                        chain.then(V.scalar_tensor_tensor(out=y[:, i, :], in0=o[:, 0, 0:C], scalar=rden[:, i, 0:1], in1=bo_rows[:, :],
                                                          op0=ALU.mult, op1=ALU.add))
                        V.scalar_tensor_tensor(out=y[:, i, :], in0=o[:, 1, 0:C], scalar=rden[:, i, 1:2], in1=y[:, i, :],
                                               op0=ALU.mult, op1=ALU.add).then_inc(S["y_rows"], 1)
                    elif step == "xt":
                        V.tensor_copy(xt[:, 4 * i:4 * i + 4, :].rearrange("p t n -> p (t n)"), filled("xt", i)[:, :]).then_inc(S["ffn_by_D"], 1)
                    elif step == "logits":
                        V.tensor_copy(lg[:, :], filled("logits")[:, 0:E]).then_inc(S["ffn_by_D"], 1)
                        dve.wait_ge(S["ffn_by_D"], evacuated_by("D", FILL_AT["logits"]))
                    elif step == "top2":
                        top2(chain, i)
                    elif step in ("route", "droute"):
                        bank = filled(step)
                        first = 0 if step == "route" else 2
                        V.tensor_scalar(ohA[:, :, :].rearrange("e k n -> e (k n)"), bank[:, 0:2 * P], unscale[:, first:first + 1], None, ALU.mult)
                        V.tensor_scalar(ohB[:, :, :].rearrange("e k n -> e (k n)"), bank[:, 0:2 * P], unscale[:, first + 1:first + 2], None, ALU.mult)
                        n = G if step == "route" else P
                        V.tensor_copy(pb[:, 0:n], bank[:, 2 * P:2 * P + n]).then_inc(S["ffn_by_D"], 1)
                        dve.wait_ge(S["ffn_by_D"], evacuated_by("D", FILL_AT[step]))
                    elif step in ("gather_b", "gather_a", "dgather_a", "dgather_b"):
                        if FILL_BY[FILL_AT[step] + i] == "D":
                            evacuate_gather(dve, "D", V.tensor_copy, step, i, gb if step in ("gather_b", "dgather_a") else ga)
                    elif step == "xbd" and i % 2 == 0:
                        V.tensor_copy(*x_block(2 * i + 1)).then_inc(S["xbd_by_dve"], 1)
                    elif step == "stage1":
                        V.tensor_tensor(tok[:, 8 * i:8 * i + 8, :], filled("stage1", i)[:, :].rearrange("q (g p) -> q g p", g=8),
                                        pb[:, 8 * i:8 * i + 8].unsqueeze(2).broadcast_to([P, 8, F1]), ALU.mult).then_inc(S["ffn_by_D"], 1)
                    elif step == "stage2" and i >= 1:
                        V.tensor_tensor(tok[:, 8 * i - 8:8 * i, :], filled("stage2", i - 1)[:, :].rearrange("q (g p) -> q g p", g=8),
                                        bup[:, :].unsqueeze(1).broadcast_to([P, 8, F1]), ALU.add).then_inc(S["ffn_by_D"], 1)
                    elif step == "dlogits" and i == 7:
                        for h in range(2):
                            V.tensor_copy(lg[G * h:G * h + G, :], filled("dlogits", h)[G * h:G * h + G, 0:E]).then_inc(S["ffn_by_D"], 1)
                        dve.wait_ge(S["ffn_by_D"], evacuated_by("D", FILL_AT["dlogits"] + 1))
                    elif step == "dstage1" and i >= 1:
                        V.tensor_tensor(tok[:, 8 * i - 8:8 * i, :].rearrange("q g (k o) -> q g k o", k=2),
                                        filled("dstage1", i - 1)[:, :].rearrange("q (g k o) -> q g k o", g=8, k=2),
                                        pb[:, :].rearrange("q (k g) -> q g k", k=2)[:, 8 * i - 8:8 * i].unsqueeze(3).broadcast_to([P, 8, 2, D1]),
                                        ALU.mult).then_inc(S["ffn_by_D"], 1)
                meet(dve, "dve")

            iterations(dve, run)

        @block.tensor
        def _(pe):
            M = nc.tensor.matmul
            pe.wait_ge(s_attw, 80)
            open_banks = {}

            def begin(stage, i=0):
                fill = FILL_AT[stage] + i
                if fill >= 4:
                    evacuated(fill - 4)
                return banks[4 + fill % 4]

            def evacuated(fill):
                for who in "AD":
                    if evacuated_by(who, fill):
                        pe.wait_ge(S[f"ffn_by_{who}"], evacuated_by(who, fill))

            def gather(stage, i, table, hot):
                bank = begin(stage, i)
                if stage[0] == "d":
                    for e in range(4):
                        for h in range(2):
                            last = M(bank[G * h:G * h + G, e * P:(e + 1) * P], table[:, (4 * i + e) * F1:(4 * i + e + 1) * F1],
                                     hot[:, :, G * h:G * h + G], start=True, stop=True)
                else:
                    for e in range(8):
                        for c in range(4):
                            last = M(bank[32 * c:32 * c + 32, e * G:(e + 1) * G], table[:, (8 * i + e) * D1:(8 * i + e + 1) * D1],
                                     hot[:, c % 2, G * (c // 2):G * (c // 2) + G], start=True, stop=True)
                last.then_inc(S["ffn_filled"], 1)

            def per_token(stage, s, left, right):
                if s < 8:
                    open_banks[s] = begin(stage, s)
                for g in range(8):
                    if s < 8:
                        M(open_banks[s][0:G, g * F1:(g + 1) * F1], left[0:G, 8 * s + g, :], right[0:G, 8 * s + g, :], start=True, stop=True)
                    if s >= 1:
                        last = M(open_banks[s - 1][G:P, g * F1:(g + 1) * F1], left[G:P, 8 * s - 8 + g, :], right[G:P, 8 * s - 8 + g, :],
                                 start=True, stop=True)
                if s >= 1:
                    last.then_inc(S["ffn_filled"], 1)

            def run(b, steps):
                if steps is FIRST:
                    pe.wait_ge(s_ffnw, 80)
                    pe.wait_ge(s_tabs, 1)
                for step, i in steps:
                    if step == "xnT":
                        if i == 0:
                            pe.wait_ge(S["norm_applied"], norm_count(steps, "norm1"))
                            if ("scores", 0) in steps:
                                pe.wait_ge(S["probs_ready"], UNITS * T)
                        for t in range(4):
                            last = nc.tensor.transpose(banks[i][:, P * t:P * t + P], xn[:, 4 * i + t, :], ident)
                        last.then_inc(S["att_filled"], 1)
                    elif step == "qkv":
                        if i == 0:
                            pe.wait_ge(S["xnT_by_act"], 1)
                            pe.wait_ge(S["xnT_by_dve"], 1)
                        if i >= 4:
                            pe.wait_ge(S["qkv_ready"], i - 3)
                        elif ("wo", 0) in steps:
                            pe.wait_ge(S["y_rows"], 5 + i)
                        M(banks[(2 + i) % 4][:, 0:3 * C], xnT[:, i * P:(i + 1) * P], wqkv[:, :], start=True, stop=True)\
                            .then_inc(S["att_filled"], 1)
                    elif step == "qkT":
                        pe.wait_ge(S["qkv_ready"], T)
                        if i >= 2:
                            pe.wait_ge(S["qk_scaled"], i - 1)
                        for t in range(4):
                            last = nc.tensor.transpose(banks[(2 + i) % 4][:, P * t:P * t + P], qk[:, 4 * (i % 2) + t, C * (1 - i // 2):C * (2 - i // 2)], ident)
                        last.then_inc(S["att_filled"], 1)
                    elif step == "scores":
                        u, kt = divmod(i, T)
                        h, qh = divmod(u, QH)
                        if i >= 2:
                            pe.wait_ge(S["probs_ready"], i - 1)
                        M(banks[kt % 2][:, :], kT[h * DH:(h + 1) * DH, kt * P:(kt + 1) * P],
                          qT[h * DH:(h + 1) * DH, qh * BANK:(qh + 1) * BANK], start=True, stop=True).then_inc(S["scores_filled"], 1)
                    elif step == "values":
                        u, kt = divmod(i, T)
                        h = u // QH
                        if kt == 0 and u >= 2:
                            pe.wait_ge(S["oT_by_act"] if u % 2 == 0 else S["oT_by_dve"], u // 2)
                        pe.wait_ge(S["probs_ready"], i + 1)
                        M(banks[2 + u % 2][0:OROWS, :], vv_flat[:, kt, h * DH:h * DH + OROWS], pT[:, u % 2, kt, :],
                          start=(kt == 0), stop=(kt == T - 1)).then_inc(S["pv_filled"], 1)
                    elif step == "wo":
                        if i == 0:
                            pe.wait_ge(S["oT_by_act"], UNITS // 2)
                            pe.wait_ge(S["oT_by_dve"], UNITS // 2)
                        if i in (2, 3) and ("xnT", 0) in steps:
                            pe.wait_ge(S["xnT_by_act"] if i == 2 else S["xnT_by_dve"], 1)
                        if i >= 4:
                            pe.wait_ge(S["y_rows"], i - 3)
                        for h in range(HEADS):
                            last = M(banks[(2 + i) % 4][:, h * (C + 1):(h + 1) * (C + 1)], oT[0:OROWS, h * QH + i // 4, (i % 4) * P:(i % 4 + 1) * P],
                                     wo[:, h, :], start=True, stop=True)
                        last.then_inc(S["att_filled"], 1)
                    elif step == "xt":
                        bank = begin("xt", i)
                        for t in range(4):
                            last = nc.tensor.transpose(bank[:, P * t:P * t + P], x2n[:, 4 * i + t, :], ident)
                        last.then_inc(S["ffn_filled"], 1)
                    elif step == "logits":
                        evacuated(FILL_AT["xt"] + 1)
                        bank = begin("logits")
                        for t in range(T):
                            last = M(bank[:, 0:E], xt[:, t, :], wup[:, t, :], start=(t == 0), stop=(t == T - 1))
                        last.then_inc(S["ffn_filled"], 1)
                    elif step in ("route", "droute"):
                        pe.wait_ge(S["route_ready"], 1 if step == "route" else 2)
                        bank = begin(step)
                        for k in range(2):
                            nc.tensor.transpose(bank[:, k * P:(k + 1) * P], oh[:, k, :], ident)
                        if step == "route":
                            last = M(bank[:, 2 * P:2 * P + G], spread[:, 0:P], mask_g, start=True, stop=True)
                        else:
                            last = M(bank[:, 2 * P:3 * P], mask_half, spread[:, 0:P], start=True, stop=True)
                        last.then_inc(S["ffn_filled"], 1)
                    elif step in ("gather_b", "dgather_a"):
                        if i == 0:
                            evacuated(FILL_AT["route" if step == "gather_b" else "droute"])
                        gather(step, i, *((tab[1], ohB) if step == "gather_b" else (tab[2], ohA)))
                    elif step in ("gather_a", "dgather_b"):
                        gather(step, i, *((tab[0], ohA) if step == "gather_a" else (tab[3], ohB)))
                    elif step == "stage1":
                        if i == 0:
                            evacuated(FILL_AT["gather_b"] + 7)
                            pe.wait_ge(S["xbd_by_act"], 8)
                            pe.wait_ge(S["xbd_by_dve"], 4)
                            pe.wait_ge(S["xbd_by_pool"], 4)
                        bank = begin("stage1", i)
                        for g in range(8):
                            last = M(bank[:, g * F1:(g + 1) * F1], xbd[:, 8 * i + g, :], gb[:, 8 * i + g, :], start=True, stop=True)
                        last.then_inc(S["ffn_filled"], 1)
                    elif step == "stage2":
                        if i == 0:
                            evacuated(FILL_AT["gather_a"] + 7)
                        per_token(step, i, ga, tok)
                    elif step == "dlogits":
                        if i == 0:
                            pe.wait_ge(S["hidden_ready"], 8)
                            for h in range(2):
                                open_banks[h] = begin(step, h)
                        for p in range(8 * i, 8 * i + 8):
                            for h in range(2):
                                last = M(open_banks[h][G * h:G * h + G, 0:E], tok[G * h:G * h + G, :, p], wdn[G * h:G * h + G, p, :],
                                         start=(p == 0), stop=(p == F1 - 1))
                                if p == F1 - 1:
                                    last.then_inc(S["ffn_filled"], 1)
                    elif step == "dstage1":
                        if i == 0:
                            evacuated(FILL_AT["dgather_b"] + 7)
                        per_token(step, i, tok, gb)
                    elif step == "dstage2":
                        if i == 0:
                            evacuated(FILL_AT["dstage1"] + 7)
                            for h in range(2):
                                open_banks[h] = begin(step, h)
                        for g in range(8 * i, 8 * i + 8):
                            for h in range(2):
                                for k in range(2):
                                    last = M(open_banks[h][32 * (g % 4):32 * (g % 4) + 32, (g // 4) * D1:(g // 4 + 1) * D1],
                                             tok[G * h:G * h + G, g, k * D1:(k + 1) * D1], ga[G * h:G * h + G, g, k * D1:(k + 1) * D1],
                                             start=(k == 0), stop=(k == 1))
                                if g == G - 1:
                                    last.then_inc(S["ffn_filled"], 1)
                meet(pe, "pe")

            iterations(pe, run)


def kernel(L0_attn_x, L0_attn_Wq, L0_attn_Wk, L0_attn_Wv, L0_attn_Wo, L0_attn_bo, L0_attn_ln_g, L0_attn_ln_b,
           L0_attn_q_gamma, L0_attn_k_gamma, L0_ffn_W_up, L0_ffn_A_up, L0_ffn_B_up, L0_ffn_scale_up, L0_ffn_bias_up,
           L0_ffn_W_down, L0_ffn_A_down, L0_ffn_B_down, L0_ffn_scale_down, L0_ffn_bias_down):
    import concourse.bacc as bacc
    from concourse.bass_utils import run_bass_kernel_spmd

    a = {k: np.asarray(v) for k, v in locals().items() if k.startswith("L0_")}

    def rows(v):
        return np.ascontiguousarray(np.broadcast_to(v.reshape(1, -1), (P, v.size)))

    n = np.arange(P)
    shape_consts = np.concatenate([
        np.eye(P), np.broadcast_to(n % E, (P, P)), (n[:, None] // G == n[None, :] // G),
        (n[:, None] % G == np.arange(G)[None, :]), -(n[:, None] >= E).astype(float)], axis=1).astype(np.float32)
    w_down = a["L0_ffn_W_down"].reshape(E, F1, F1).transpose(1, 2, 0)
    bias_up = a["L0_ffn_bias_up"].reshape(F1, F1)
    w_o = np.zeros((OROWS, HEADS, C + 1), np.float32)
    w_o[0:DH, 0, 0:C], w_o[ONES:OROWS, 1, 0:C] = a["L0_attn_Wo"].T[0:DH], a["L0_attn_Wo"].T[DH:C]
    w_o[DH, 0, C] = w_o[0, 1, C] = 1.0
    ins = {
        "x": a["L0_attn_x"],
        "w_qkv": np.concatenate([a["L0_attn_Wq"].T, a["L0_attn_Wk"].T, a["L0_attn_Wv"].T], axis=1),
        "w_o": w_o,
        "bo": rows(a["L0_attn_bo"]),
        "ln_gamma": np.stack([a["L0_attn_ln_g"], a["L0_attn_ln_b"], np.tile(a["L0_attn_q_gamma"], HEADS),
                              np.tile(a["L0_attn_k_gamma"], HEADS)], axis=1),
        "a_up": a["L0_ffn_A_up"].reshape(E, -1),
        "b_up": a["L0_ffn_B_up"].reshape(E, -1),
        "a_down": a["L0_ffn_A_down"].reshape(E, -1),
        "b_down": a["L0_ffn_B_down"].reshape(E, -1),
        "w_up": a["L0_ffn_W_up"].reshape(E, T, C).transpose(2, 1, 0),
        "w_down": np.concatenate([w_down, w_down], axis=0),
        "bias_up": np.concatenate([bias_up, bias_up], axis=0),
        "bias_down": rows(a["L0_ffn_bias_down"]),
        "scales": np.concatenate([rows(a["L0_ffn_scale_up"]), rows(a["L0_ffn_scale_down"])], axis=1),
        "shape_consts": shape_consts,
    }
    ins = {k: np.ascontiguousarray(v) for k, v in ins.items()}
    nc = bacc.Bacc("TRN2", target_bir_lowering=False, num_devices=1)
    h = {k: nc.dram_tensor(f"in_{k}", v.shape, mybir.dt.from_np(v.dtype), kind="ExternalInput").ap() for k, v in ins.items()}
    out = nc.dram_tensor("out", (B, N, C), F32, kind="ExternalOutput").ap()
    tables = [h.pop(k) for k in ("a_up", "b_up", "a_down", "b_down")]
    build_program(nc, tables=tables, out=out, **h)
    r = run_bass_kernel_spmd(nc, [{f"in_{k}": v for k, v in ins.items()}], core_ids=[0])
    return r.results[0]["out"]
```

```python
from contextlib import ExitStack

import numpy as np

import concourse.bass as bass
from concourse import mybir

ALU = mybir.AluOpType
ACT = mybir.ActivationFunctionType
AX = mybir.AxisListType
F32 = mybir.dt.float32
F16 = mybir.dt.float16
BF16 = mybir.dt.bfloat16
I32 = mybir.dt.int32
U32 = mybir.dt.uint32

P = 128
B, N, C = 8, 1024, 128
HEADS, DH = 2, 64
ONES = 32
OROWS = DH + ONES
T = N // P
E = 64
D1, F1 = 32, 64
G = P // 2
BANK = 512
QH = N // BANK
UNITS = HEADS * QH
EPS = 1e-5
RMS_FLOOR = 1e-16
K_UP, Q_UP = 2.0 ** 10, 2.0 ** 10
EXP_TOP = 80.0


class Count:

    def __init__(self, eng, sem):
        self.eng, self.sem, self.n = eng, sem, 0

    def __call__(self, instruction):
        self.n += 1
        return instruction.then_inc(self.sem, 1)

    def settle(self):
        self.eng.wait_ge(self.sem, self.n)

    def then(self, instruction):
        self(instruction)
        self.settle()


FFN_FILLS = [
    ("xt", 2, "DD"), ("logits", 1, "D"), ("route", 1, "D"),
    ("gather_b", 8, "ADADADAD"), ("stage1", 8, "DDDDDDDD"), ("gather_a", 8, "ADADADAD"), ("stage2", 8, "DDDDDDDD"),
    ("dlogits", 2, "DD"), ("droute", 1, "D"),
    ("dgather_a", 8, "AAAAAAAA"), ("dgather_b", 8, "AAAAAAAA"), ("dstage1", 8, "DDDDDDDD"), ("dstage2", 2, "AA"),
]
FILL_AT, FILL_BY = {}, []
for _name, _n, _by in FFN_FILLS:
    FILL_AT[_name] = len(FILL_BY)
    FILL_BY += list(_by)


def evacuated_by(engine, fill):
    return FILL_BY[:fill + 1].count(engine)


def s_(*n):
    return [("scores", i) for i in n]


def v_(*n):
    return [("values", i) for i in n]


def interleave(stage, count, between):
    steps = []
    for i in range(count):
        steps += [(stage, i)] + (between[i] if i < len(between) else [])
    return steps


STEADY = s_(0, 1) + [("xt", 0), ("xt", 1)] + s_(2, 3) + [("logits", 0), ("top2", 0)] + s_(4) + v_(0, 1) + s_(5, 6) + [("route", 0)] + v_(2, 3)
STEADY += interleave("gather_b", 8, [[("xbd", 0)] + s_(7) + v_(4), [("xbd", 1)], [("xbd", 2)], [("xbd", 3)] + s_(8), [("xbd", 4)],
                                     s_(9) + [("xbd", 5)] + v_(5) + s_(10) + v_(6), [("xbd", 6)], [("xbd", 7)]])
STEADY += v_(7, 8) + [("end", 0)]
STEADY += interleave("stage1", 8, [[], [], s_(11) + [("end", 1), ("end", 2)], [("end", 3)], [("end", 4)], [], v_(9)])
STEADY += interleave("gather_a", 8, [[("seed", 0)], [], s_(12) + v_(10), [], s_(13), [], s_(14, 15) + v_(11, 12)])
STEADY += s_(16, 17) + v_(13)
STEADY += interleave("stage2", 9, [[], s_(18, 19), s_(20, 21) + [("norm1", 0), ("norm1", 1)] + v_(14), [],
                                   s_(22, 23) + v_(15) + [("gelu", 0), ("gelu", 1), ("gelu", 2)], [("gelu", 3)], [("gelu", 4)],
                                   v_(16, 17, 18) + [("gelu", 5)]])
STEADY += [("gelu", 6), ("gelu", 7)] + s_(24) + v_(19) + [("norm1", 2)] + s_(25) + v_(20, 21)
STEADY += interleave("dlogits", 8, [[], [], v_(22, 23), [], s_(26), v_(24), [("norm1", 3)] + s_(27) + v_(25, 26)])
STEADY += s_(28) + [("top2", 1)] + s_(29) + v_(27, 28) + s_(30, 31) + [("droute", 0)] + v_(29, 30)
STEADY += interleave("dgather_a", 8, [[], [], [], [], v_(31) + [("xnT", 0), ("xnT", 1)]])
STEADY += interleave("dgather_b", 8, [[("wo", 0)], [], [], [("wo", 1), ("wo", 2), ("wo", 3)], [], [("wo", 4), ("wo", 5)]])
STEADY += [("wo", 6), ("wo", 7), ("qkv", 0)]
STEADY += interleave("dstage1", 9, [[], [("qkv", 1), ("qkv", 2), ("norm_y", 0)], [("qkv", 3), ("qkv", 4)], [("norm_y", 1)],
                                    [("qkv", 5), ("norm_y", 2)], [], [("qkv", 6)]])
STEADY += [("norm_y", 3), ("qkv", 7)]
STEADY += interleave("dstage2", 8, [[], [("rms", 0)], [("norm_y", 4)], [("norm2", 0), ("qkT", 0), ("qkT", 1), ("qkT", 2)],
                                    [("norm2", 1), ("qkT", 3), ("qkT", 4), ("norm2", 2)], [("qkT", 5), ("qkT", 6)], [("norm2", 3), ("qkT", 7)]])
STEADY += [("qkT", 8), ("qkT", 9), ("qkT", 10), ("qkT", 11)]
FRONT = {"norm1", "xnT", "qkv", "rms", "qkT"}
BACK = {"scores", "values", "wo", "norm_y", "norm2"}
START = [s for s in STEADY if s[0] in FRONT]
START.insert(START.index(("norm1", 1)) + 1, ("setup", 0))
PROLOGUE = [s for s in STEADY if s[0] in FRONT | BACK | {"seed"}]
for _i, _after in enumerate([("scores", 0), ("scores", 1), ("values", 12), ("values", 18)]):
    PROLOGUE.insert(PROLOGUE.index(_after) + 1, ("tables", _i))
FIRST = [s for s in STEADY if s[0] != "end"]
SHORT = [s for s in STEADY if s[0] not in FRONT]
LAST = [s for s in STEADY if s[0] not in FRONT | BACK]
END = [("end", i) for i in range(5)]
ATT_FILLS = {"xnT", "wo", "qkv", "qkT"}


NORMS = {"norm1", "norm_y", "norm2", "end"}
NORM_SLOT = {"norm1": 0, "norm_y": 1, "norm2": 2, "end": 3}


def norm_count(steps, step):
    return [s[0] for s in steps if s[0] in NORMS and s[1] == 3].index(step) + 1


QKT = [(a, h, half) for a in ("k", "q", "q_swapped") for h in range(HEADS) for half in range(2)]


def att_fill(steps, step, i):
    return [s for s in steps if s[0] in ATT_FILLS].index((step, i)) + 1


def build_program(nc, x, w_qkv, w_o, bo, ln_affine, gammas, tables, w_up, w_down, bias_up, bias_down, scales, shape_consts, out):
    with ExitStack() as ctx:
        def sb(name, shape, dt=F32):
            return ctx.enter_context(nc.sbuf_tensor(name, shape, dt))

        wqkv = sb("wqkv", [P, 3 * C])
        wo = sb("wo", [OROWS, HEADS, C + 1])
        bo_rows = sb("bo_rows", [P, C])
        gam = sb("gam", [P, 2])
        gqk = sb("gqk", [P, C])
        wup = sb("wup", [P, T, E])
        wdn = sb("wdn", [P, F1, E])
        bup = sb("bup", [P, F1])
        bdn = sb("bdn", [P, N])
        scl = sb("scl", [P, 2])
        tab = [sb(f"tab{i}", [P, 2048], F16) for i in range(4)]
        unscale = sb("unscale", [P, 4])
        cst = sb("cst", [P, 3 * P + G + 1])
        ident, iota = cst[:, 0:P], cst[:, P:2 * P]
        mask_half, mask_g = cst[:, 2 * P:3 * P], cst[:, 3 * P:3 * P + G]
        mask_low = cst[:, 3 * P + G:3 * P + G + 1]
        shift = sb("shift", [P, 2])
        ident16 = sb("ident16", [P, P], F16)

        xin = sb("xin", [P, T, C])
        xn = sb("xn", [P, T, C])
        qk = sb("qk", [P, T, 2 * C])
        vv = sb("vv", [P, T * (OROWS + DH) + ONES])
        kT = sb("kT", [P, HEADS, N], F16)
        qT = sb("qT", [P, HEADS, N], F16)
        qT_swapped = sb("qT_swapped", [P, HEADS, N], F16)
        pT = sb("pT", [P, 2, T, BANK])
        y = pT[:, 0, 0:2, :].rearrange("p a b -> p (a b)").rearrange("p (t c) -> p t c", t=T)
        sq = pT[:, 1, 0:4, :].rearrange("p a b -> p (a b)").rearrange("p (t c) -> p t c", t=T)
        split = pT[:, 0, 3:8, :].rearrange("p a b -> p (a b)").bitcast(F16).rearrange("p (t c) -> p t c", t=T)
        k_split = split[:, :, 0:4 * DH].rearrange("p t (h s d) -> p t h s d", h=HEADS, s=2)
        q_split = split[:, :, 4 * DH:10 * DH].rearrange("p t (h s d) -> p t h s d", h=HEADS, s=3)
        oT = qk[:, :, :].rearrange("p a b -> p (a b)").rearrange("p (u n) -> p u n", u=UNITS)

        x2 = sb("x2", [P, T, C])
        x2n = sb("x2n", [P, T, C])
        x2_old = sb("x2_old", [P, T, C])
        ydn = x2n
        xt = sb("xt", [P, T, P])
        xnT = xt[:, :, :].rearrange("p t n -> p (t n)")
        ys = xn[:, :, :].rearrange("p a b -> p (a b)")
        xbd = sb("xbd", [P, G, P])
        stage = xbd[:, :, :].rearrange("p a b -> p (a b)").rearrange("p (i n) -> p i n", i=4)
        gb = sb("gb", [P, G, F1])
        ga = sb("ga", [P, G, F1])
        tok = sb("tok", [P, G, F1])
        lg = ga[:, 6, :]
        m8, i8, idx, gap, prob = ga[:, 7, 0:8], ga[:, 7, 8:16].bitcast(U32), ga[:, 7, 16:18], ga[:, 7, 18:22], ga[:, 7, 22:24]
        oh = ga[:, 0:4, :].rearrange("p a b -> p (a b)").rearrange("p (k n) -> p k n", k=2)
        spread = ga[:, 4:6, :].rearrange("p a b -> p (a b)")
        ohA = sb("ohA", [P, 2, P], BF16)
        ohB = sb("ohB", [P, 2, P], BF16)
        pb = sb("pb", [P, P])

        bn = sb("bn", [P, T, 6])
        mv = sb("mv", [P, T, 2])
        factor = sb("factor", [P, len(NORMS), 2, T])
        ssq = sb("ssq", [P, 4 * T])
        rs = sb("rs", [P, 4 * T])
        rms = rs[:, 0:4 * T].rearrange("p (t m) -> p t m", t=T)
        rt = sb("rt", [P, 4 * T])
        rv = sb("rv", [P, 4 * T])
        rden = sb("rden", [P, T, HEADS])
        gamma_rows = ga[:, 8:12, :].rearrange("p a b -> p (a b)").rearrange("p (k c) -> p k c", k=2)
        ms, bits = ga[:, 0, 0:4], ga[:, 0, 4:6].bitcast(I32)

        banks = [ctx.enter_context(nc.psum_tensor(f"bank{i}", [P, BANK], F32)) for i in range(8)]

        def sem(name):
            return ctx.enter_context(nc.semaphore(name))

        s_attw, s_ffnw = sem("attention_weights_loaded"), sem("ffn_weights_loaded")
        s_tab = [sem(f"table{i}_loaded") for i in range(4)]
        s_setup, s_tabs, s_setchain = sem("setup_done"), sem("tables_split"), sem("setup_chain")
        s_done, s_go = sem("engines_done"), {k: sem(f"go_{k}") for k in ("sp", "act", "pe", "dve")}
        names = ["x_loaded", "norm_ready", "norm_applied", "att_filled", "xnT_by_act", "xnT_by_dve", "qkv_ready", "squares_ready",
                 "rms_ready", "q_scaled", "k_scaled", "high_ready", "split_ready", "qkT_by_act", "qkT_by_dve", "scores_filled", "probs_ready", "pv_filled", "oT_by_act", "oT_by_dve",
                 "y_rows", "ffn_filled", "ffn_by_A", "ffn_by_D", "xbd_by_act", "xbd_by_dve", "xbd_by_pool", "gap_ready", "gap_exp",
                 "hidden_ready", "route_ready", "ys_stored", "y_loaded", "out_ready", "out_stored", "x2_kept", "x2_seeded", "dve_chain"]
        S = {n: sem(n) for n in names}
        nums = sorted(S[n].num for n in names)
        assert nums == list(range(nums[0], nums[0] + len(names)))

        scratch = nc.dram_tensor("y_scratch", [P, N], F32).ap()
        x_v = x.rearrange("b (p t) c -> (b p) t c", t=T)
        out_v = out.rearrange("b (p t) c -> (b p) t c", t=T)

        block = ctx.enter_context(nc.Block())

        def normed(step):
            return {"norm1": (xn, xin), "norm_y": (y, y), "norm2": (x2n, x2), "end": (ydn, ydn)}[step]

        def v_tile(t):
            at = t * (OROWS + DH)
            return vv[:, at:at + 2 * OROWS].rearrange("p (h d) -> p h d", h=HEADS)[:, :, 0:DH]

        def qkT_part(i):
            array, h, half = QKT[i]
            return {"k": kT, "q": qT, "q_swapped": qT_swapped}[array][:, h, half * BANK:half * BANK + BANK]

        def x_block(n):
            cb, c = divmod(n, 4)
            return (xbd[32 * c:32 * c + 32, :, 32 * c + cb:32 * c + 32:4].rearrange("j g t -> j t g"),
                    xt[32 * cb:32 * cb + 32, :, G * (c // 2):G * (c // 2) + G])

        def evacuate_gather(eng, who, copy, stage, i, dst):
            fill = FILL_AT[stage] + i
            eng.wait_ge(S["ffn_filled"], fill + 1)
            bank = banks[4 + fill % 4]
            if stage[0] == "d":
                src = bank[:, :].rearrange("q (e k g) -> q e k g", e=4, k=2)
                to = dst[:, :, :].rearrange("q g (k e) -> q e k g", k=2)[:, 4 * i:4 * i + 4]
                for k in range(2):
                    last = copy(to[:, :, k], src[:, :, k])
            else:
                last = copy(dst[:, :, :].rearrange("q g e -> q e g")[:, 8 * i:8 * i + 8], bank[:, :].rearrange("q (e g) -> q e g", e=8))
            last.then_inc(S[f"ffn_by_{who}"], 1)

        def iterations(eng, run):
            run(-2, START)
            run(-1, PROLOGUE)
            run(0, FIRST)
            with eng.Fori(1, B - 2) as b:
                run(b, STEADY)
            run(B - 2, SHORT)
            run(B - 1, LAST)
            run(B, END)

        def meet(eng, name):
            eng.drain().then_inc(s_done, 1)
            eng.wait_ge(s_go[name], 1)
            eng.sem_clear(s_go[name])

        @block.sync
        def _(sp):
            def load_x(b):
                sp.dma_start(xin[:, :, :], x_v[bass.ds(b * P, P)]).then_inc(S["x_loaded"], 16)

            def run(b, steps):
                if steps is START:
                    load_x(0)
                    for dst, src in [(cst[:, :], shape_consts), (gam[:, :], ln_affine), (gamma_rows[:, :, :], gammas), (wqkv[:, :], w_qkv), (wo[:, :, :], w_o),
                                     (bo_rows[:, :], bo)]:
                        sp.dma_start(dst, src).then_inc(s_attw, 16)
                    for i in range(4):
                        for half in range(2):
                            sp.dma_start(stage[half * E:(half + 1) * E, i, :], tables[i]).then_inc(s_tab[i], 16)
                    for dst, src in [(wup[:, :, :], w_up), (wdn[:, :, :], w_down), (bup[:, :], bias_up), (bdn[:, :], bias_down),
                                     (scl[:, :], scales)]:
                        sp.dma_start(dst, src).then_inc(s_ffnw, 16)
                    sp.wait_ge(s_ffnw, 80)
                if ("end", 0) in steps:
                    for c in range(4):
                        sp.dma_start(scratch.rearrange("(s c) (o p) -> c o s p", c=4, p=D1)[c],
                                     ys[c * D1:(c + 1) * D1, :].rearrange("o (s p) -> o s p", p=D1)).then_inc(S["ys_stored"], 16)
                    sp.wait_ge(S["ys_stored"], 64)
                    if ("xt", 0) in steps:
                        sp.wait_ge(S["ffn_filled"], FILL_AT["xt"] + 2)
                    sp.dma_start(ydn[:, :, :], scratch.rearrange("n (t c) -> n t c", t=T)).then_inc(S["y_loaded"], 16)
                    sp.wait_ge(S["out_ready"], 1)
                    sp.dma_start(out_v[bass.ds((b - 1) * P, P)], ydn[:, :, :]).then_inc(S["out_stored"], 16)
                if ("norm1", 0) in steps and steps is not START:
                    sp.wait_ge(S["x2_seeded"], 1)
                    load_x(b + 2)
                if ("end", 0) in steps:
                    sp.wait_ge(S["out_stored"], 16)
                meet(sp, "sp")

            iterations(sp, run)

        @block.gpsimd
        def _(pool):
            def run(b, steps):
                for step, i in steps:
                    if step == "xbd" and i % 2 == 1:
                        pool.wait_ge(S["ffn_by_D"], 2)
                        if i > 1:
                            pool.wait_ge(S["xbd_by_pool"], i // 2)
                        dst, src = x_block(2 * i + 1)
                        nc.gpsimd.tensor_scalar(dst, src, 1.0, None, ALU.mult).then_inc(S["xbd_by_pool"], 1)
                    elif step == "rms":
                        pool.wait_ge(S["rms_ready"], 1)
                        k = qk[:, :, C:2 * C].rearrange("p t (h d) -> p t h d", h=HEADS)
                        nc.gpsimd.tensor_tensor(k, k, rms[:, :, HEADS:2 * HEADS].unsqueeze(3).broadcast_to([P, T, HEADS, DH]), ALU.mult)\
                            .then_inc(S["k_scaled"], 1)
                pool.drain()
                pool.wait_ge(s_done, 4)
                pool.sem_clear(range(nums[0], nums[0] + len(names)))
                pool.sem_clear(s_done)
                for k in ("sp", "act", "pe", "dve"):
                    pool.sem_inc(s_go[k], 1)

            iterations(pool, run)

        @block.scalar
        def _(act):
            A = nc.scalar
            act.wait_ge(s_attw, 96)

            def copy(dst, src):
                return A.activation(dst, src, ACT.Copy)

            def run(b, steps):
                for step, i in steps:
                    if step == "xnT" and i == 0:
                        act.wait_ge(S["att_filled"], att_fill(steps, step, i))
                        A.activation(xnT[:, 0:BANK], banks[0][:, :], ACT.Identity, bias=gam[:, 1:2], scale=gam[:, 0:1])\
                            .then_inc(S["xnT_by_act"], 1)
                    elif step == "qkv":
                        act.wait_ge(S["att_filled"], att_fill(steps, step, i))
                        bank = banks[(2 + i) % 4]
                        A.activation(sq[:, i, :], bank[:, 0:2 * C], ACT.Square).then_inc(S["squares_ready"], 1)
                        copy(qk[:, i, :], bank[:, 0:2 * C])
                        copy(v_tile(i), bank[:, 2 * C:3 * C].rearrange("p (h d) -> p h d", h=HEADS)).then_inc(S["qkv_ready"], 1)
                    elif step == "rms":
                        act.wait_ge(S["k_scaled"], 1)
                        copy(k_split[:, :, :, 0], qk[:, :, C:2 * C].rearrange("p t (h d) -> p t h d", h=HEADS)).then_inc(S["high_ready"], 1)
                        act.wait_ge(S["q_scaled"], 1)
                        for part in (0, 2):
                            copy(q_split[:, :, :, part], qk[:, :, 0:C].rearrange("p t (h d) -> p t h d", h=HEADS)).then_inc(S["high_ready"], 1)
                    elif step == "qkT" and i % 2 == 0:
                        act.wait_ge(S["att_filled"], att_fill(steps, step, i))
                        copy(qkT_part(i), banks[(2 + i) % 4][:, :]).then_inc(S["qkT_by_act"], 1)
                    elif step == "scores":
                        u, kt = divmod(i, T)
                        if steps is PROLOGUE and i == 0:
                            act.wait_ge(s_setup, 1)
                        if u >= 2:
                            act.wait_ge(S["pv_filled"], i + 1 - 2 * T)
                        act.wait_ge(S["scores_filled"], i + 1)
                        A.activation(pT[:, u % 2, kt, :], banks[kt % 2][:, :], ACT.Exp, bias=shift[:, 0:1],
                                     scale=shift[:, 1:2]).then_inc(S["probs_ready"], 1)
                    elif step == "values" and i % (2 * T) == T - 1:
                        u = i // T
                        act.wait_ge(S["pv_filled"], i + 1)
                        copy(oT[0:OROWS, u, :], banks[2 + u % 2][0:OROWS, :]).then_inc(S["oT_by_act"], 1)
                    elif step == "top2":
                        act.wait_ge(S["gap_ready"], i + 1)
                        A.activation(gap[:, 1:2], gap[:, 0:1], ACT.Exp).then_inc(S["gap_exp"], 1)
                    elif step in NORMS and i in (2, 3):
                        dst, src = normed(step)
                        if i == 2:
                            act.wait_ge(S["norm_ready"], norm_count(steps, step))
                        if step == "norm1" and ("end", 0) in steps:
                            act.wait_ge(S["ys_stored"], 64)
                        if step == "norm2" and ("end", 0) in steps:
                            act.wait_ge(S["out_stored"], 16)
                        for t in range(4 * i - 8, 4 * i - 4):
                            last = A.activation(dst[:, t, :], src[:, t, :], ACT.Identity, scale=factor[:, NORM_SLOT[step], 0, t:t + 1],
                                                bias=factor[:, NORM_SLOT[step], 1, t:t + 1])
                        if i == 3:
                            last.then_inc(S["norm_applied"], 1)
                    elif step == "seed":
                        if ("xt", 0) in steps:
                            if ("end", 0) in steps:
                                act.wait_ge(S["out_ready"], 1)
                            copy(x2_old[:, :, :], x2[:, :, :]).then_inc(S["x2_kept"], 1)
                        if ("wo", 0) in steps:
                            if ("xt", 0) in steps:
                                act.wait_ge(S["x2_kept"], 1)
                            copy(x2[:, :, :], xin[:, :, :]).then_inc(S["x2_seeded"], 1)
                    elif step == "xbd":
                        act.wait_ge(S["ffn_by_D"], 2)
                        copy(*x_block(2 * i)).then_inc(S["xbd_by_act"], 1)
                    elif step in ("gather_b", "gather_a", "dgather_a", "dgather_b") and FILL_BY[FILL_AT[step] + i] == "A":
                        evacuate_gather(act, "A", copy, step, i, gb if step in ("gather_b", "dgather_a") else ga)
                    elif step == "gelu":
                        act.wait_ge(S["ffn_by_D"], evacuated_by("D", FILL_AT["stage2"] + i))
                        A.activation(tok[:, 8 * i:8 * i + 8, :], tok[:, 8 * i:8 * i + 8, :], ACT.Gelu).then_inc(S["hidden_ready"], 1)
                    elif step == "dstage2" and i == 7:
                        for h in range(2):
                            fill = FILL_AT["dstage2"] + h
                            act.wait_ge(S["ffn_filled"], fill + 1)
                            A.activation(ys[:, BANK * h:BANK * h + BANK], banks[4 + fill % 4][:, :], ACT.Copy).then_inc(S["ffn_by_A"], 1)
                meet(act, "act")

            iterations(act, run)

        @block.vector
        def _(dve):
            V = nc.vector
            setup = Count(dve, s_setchain)
            def set_up():
                dve.wait_ge(s_attw, 96)
                setup(V.memset(vv[:, :], 1.0))
                setup(V.tensor_copy(ident16[:, :], ident))
                setup.then(V.tensor_tensor(gqk[:, :], gamma_rows[:, 0, :], gamma_rows[:, 1, :], ALU.mult))
                setup(V.tensor_reduce(ms[:, 0:1], gqk[:, :], AX.X, ALU.max))
                setup.then(V.tensor_reduce(ms[:, 1:2], gqk[:, :], AX.X, ALU.min))
                setup.then(V.scalar_tensor_tensor(out=ms[:, 2:3], in0=ms[:, 1:2], scalar=-1.0, in1=ms[:, 0:1], op0=ALU.mult, op1=ALU.max))
                setup.then(V.tensor_scalar(ms[:, 3:4], ms[:, 2:3], -(DH ** 0.5), EXP_TOP, ALU.mult, ALU.add))
                setup(V.tensor_scalar(shift[:, 0:1], ms[:, 3:4], 0.0, None, ALU.min))
                setup.then(V.tensor_scalar(ms[:, 0:1], ms[:, 2:3], 1e-30, None, ALU.max))
                setup.then(V.tensor_scalar(bits[:, 0:1], ms[:, 0:1].bitcast(I32), 0x7F800000, None, ALU.bitwise_and))
                setup(V.tensor_scalar(shift[:, 1:2], bits[:, 0:1].bitcast(F32), DH ** -0.5 / K_UP / Q_UP, None, ALU.mult))
                setup.then(V.tensor_scalar(ms[:, 1:2], bits[:, 0:1].bitcast(F32), 1.0 / Q_UP, None, ALU.mult))
                setup.then(V.tensor_scalar(bits[:, 1:2], ms[:, 1:2].bitcast(I32), -1, 0x7F000000, ALU.mult, ALU.add))
                V.tensor_scalar(gqk[:, :], gqk[:, :], bits[:, 1:2].bitcast(F32), None, ALU.mult).then_inc(s_setup, 1)
                dve.wait_ge(s_setup, 1)

            def split_table(i):
                dve.wait_ge(s_tab[i], 32)
                setup.then(V.tensor_reduce(ms[:, 2:3], stage[:, i, :], AX.X, ALU.max, apply_absolute_value=True))
                setup.then(V.tensor_scalar(ms[:, 3:4], ms[:, 2:3], 1e-30, None, ALU.max))
                setup.then(V.tensor_scalar(bits[:, 0:1], ms[:, 3:4].bitcast(I32), 0x7F800000, None, ALU.bitwise_and))
                setup.then(V.tensor_scalar(unscale[:, i:i + 1], bits[:, 0:1].bitcast(F32), 2.0 ** -13, None, ALU.mult))
                setup.then(V.tensor_scalar(bits[:, 1:2], unscale[:, i:i + 1].bitcast(I32), -1, 0x7F000000, ALU.mult, ALU.add))
                setup.then(V.tensor_scalar(stage[:, i, :], stage[:, i, :], bits[:, 1:2].bitcast(F32), None, ALU.mult))
                setup.then(V.tensor_copy(tab[i][:, :], stage[:, i, :]))
                setup.then(V.scalar_tensor_tensor(out=tab[i][:, :], in0=tab[i][:, :], scalar=mask_low, in1=stage[:, i, :],
                                                  op0=ALU.mult, op1=ALU.add))
                if i == 3:
                    V.memset(xbd[:, :, :], 0.0).then_inc(s_tabs, 1)

            def rsqrt(chain, n, dst):
                chain.then(V.tensor_scalar(rs[:, 0:n].bitcast(I32), rv[:, 0:n].bitcast(I32), -0.5, float(0x5F3759DF), ALU.mult, ALU.add))
                for step in range(3):
                    chain.then(V.scalar_tensor_tensor(out=rt[:, 0:n], in0=rs[:, 0:n], scalar=-0.5, in1=rs[:, 0:n], op0=ALU.mult, op1=ALU.mult))
                    chain.then(V.tensor_tensor(rt[:, 0:n], rt[:, 0:n], rv[:, 0:n], ALU.mult))
                    chain.then(V.scalar_tensor_tensor(out=dst if step == 2 else rs[:, 0:n], in0=rt[:, 0:n], scalar=1.5, in1=rs[:, 0:n],
                                                      op0=ALU.add, op1=ALU.mult))

            def statistics(chain, src):
                for t in range(T):
                    chain(V.bn_stats(bn[:, t, :], src[:, t, :]))
                chain.settle()
                for t in range(T):
                    chain(V.bn_aggr(mv[:, t, :], bn[:, t, :]))
                chain.settle()

            def factors(chain, step):
                a, c = (1.0 + EPS, EPS * EPS) if step == "norm1" else (1.0, EPS)
                chain.then(V.tensor_scalar(rv[:, 0:T], mv[:, :, 1], a, c, ALU.mult, ALU.add))
                slot = NORM_SLOT[step]
                rsqrt(chain, T, factor[:, slot, 0, :])
                V.scalar_tensor_tensor(out=factor[:, slot, 1, :], in0=mv[:, :, 0], scalar=-1.0, in1=factor[:, slot, 0, :],
                                       op0=ALU.mult, op1=ALU.mult).then_inc(S["norm_ready"], 1)

            def top2(chain, layer):
                chain.then(V.max(m8[:, :], lg[:, :]))
                V.tensor_tensor(gap[:, 0:1], m8[:, 1:2], m8[:, 0:1], ALU.subtract).then_inc(S["gap_ready"], 1)
                chain.then(V.max_index(i8[:, :], m8[:, :], lg[:, :]))
                chain.then(V.tensor_copy(idx[:, :], i8[:, 0:2]))
                for k in range(2):
                    chain(V.tensor_scalar(oh[:, k, :], iota, idx[:, k:k + 1], None, ALU.is_equal))
                dve.wait_ge(S["gap_exp"], layer + 1)
                chain.then(V.tensor_scalar(gap[:, 2:3], gap[:, 1:2], 1.0, None, ALU.add))
                chain.then(V.reciprocal(gap[:, 3:4], gap[:, 2:3]))
                chain.then(V.tensor_tensor(prob[:, 0:1], gap[:, 3:4], scl[:, layer:layer + 1], ALU.mult))
                chain.then(V.tensor_tensor(prob[:, 1:2], gap[:, 1:2], prob[:, 0:1], ALU.mult))
                for k in range(2):
                    if layer == 0:
                        to = spread[:, 0:P].rearrange("n (h k i) -> n h k i", h=2, k=2)[:, :, k]
                        mask = mask_half.rearrange("n (h k i) -> n h k i", h=2, k=2)[:, :, k]
                    else:
                        to, mask = spread[:, k * G:(k + 1) * G], mask_g
                    chain(V.tensor_scalar(to, mask, prob[:, k:k + 1], None, ALU.mult))
                dve.drain().then_inc(S["route_ready"], 1)

            def add_head_1(i):
                V.scalar_tensor_tensor(out=y[:, i, :], in0=banks[(2 + i) % 4][:, C + 1:2 * C + 1], scalar=rden[:, i, 1:2], in1=y[:, i, :],
                                       op0=ALU.mult, op1=ALU.add).then_inc(S["y_rows"], 1)

            def filled(stage, i=0):
                fill = FILL_AT[stage] + i
                dve.wait_ge(S["ffn_filled"], fill + 1)
                return banks[4 + fill % 4]

            def run(b, steps):
                chain = Count(dve, S["dve_chain"])
                for step, i in steps:
                    if step == "setup":
                        set_up()
                    elif step == "tables":
                        split_table(i)
                    elif step in NORMS and i == 0:
                        if step == "norm1":
                            dve.wait_ge(S["x_loaded"], 16)
                        elif step == "norm_y":
                            dve.wait_ge(S["y_rows"], T)
                        elif step == "end":
                            dve.wait_ge(S["y_loaded"], 16)
                            chain.then(V.tensor_tensor(ydn[:, :, :], ydn[:, :, :], bdn[:, :].rearrange("p (t c) -> p t c", t=T), ALU.add))
                        statistics(chain, normed(step)[1])
                    elif step in NORMS and i == 1:
                        factors(chain, step)
                    elif step == "norm_y" and i == 4:
                        dve.wait_ge(S["x2_seeded"], 1)
                        dve.wait_ge(S["norm_applied"], norm_count(steps, step))
                        chain.then(V.tensor_tensor(x2[:, :, :], x2[:, :, :], y[:, :, :], ALU.add))
                    elif step == "end" and i == 4:
                        dve.wait_ge(S["norm_applied"], norm_count(steps, step))
                        V.tensor_tensor(ydn[:, :, :], x2_old[:, :, :], ydn[:, :, :], ALU.add).then_inc(S["out_ready"], 1)
                    elif step == "xnT" and i == 1:
                        dve.wait_ge(S["att_filled"], att_fill(steps, step, i))
                        V.tensor_scalar(xnT[:, BANK:N], banks[1][:, :], gam[:, 0:1], gam[:, 1:2], ALU.mult, ALU.add)\
                            .then_inc(S["xnT_by_dve"], 1)
                    elif step == "qkv":
                        dve.wait_ge(S["squares_ready"], i + 1)
                        chain(V.tensor_reduce(ssq[:, 4 * i:4 * i + 4], sq[:, i, :].rearrange("p (m d) -> p m d", d=DH), AX.X, ALU.add))
                    elif step == "rms":
                        chain.settle()
                        dve.wait_ge(S["qkv_ready"], T)
                        chain.then(V.tensor_scalar(rv[:, 0:4 * T], ssq[:, :], 1.0 / DH, RMS_FLOOR, ALU.mult, ALU.max))
                        rsqrt(chain, 4 * T, rs[:, 0:4 * T])
                        V.tensor_scalar(rms[:, :, HEADS:2 * HEADS], rms[:, :, HEADS:2 * HEADS], K_UP, None, ALU.mult).then_inc(S["rms_ready"], 1)
                        q = qk[:, :, 0:C].rearrange("p t (h d) -> p t h d", h=HEADS)
                        chain.then(V.tensor_tensor(q, q, rms[:, :, 0:HEADS].unsqueeze(3).broadcast_to([P, T, HEADS, DH]), ALU.mult))
                        V.tensor_tensor(qk[:, :, 0:C], qk[:, :, 0:C], gqk[:, :].unsqueeze(1).broadcast_to([P, T, C]), ALU.mult)\
                            .then_inc(S["q_scaled"], 1)
                        dve.wait_ge(S["high_ready"], 1)
                        k = qk[:, :, C:2 * C].rearrange("p t (h d) -> p t h d", h=HEADS)
                        V.tensor_tensor(k_split[:, :, :, 1], k, k_split[:, :, :, 0], ALU.subtract).then_inc(S["split_ready"], 1)
                        dve.wait_ge(S["high_ready"], 2)
                        V.tensor_tensor(q_split[:, :, :, 1], q, q_split[:, :, :, 0], ALU.subtract).then_inc(S["split_ready"], 1)
                    elif step == "qkT" and i % 2 == 1:
                        dve.wait_ge(S["att_filled"], att_fill(steps, step, i))
                        V.tensor_copy(qkT_part(i), banks[(2 + i) % 4][:, :]).then_inc(S["qkT_by_dve"], 1)
                    elif step == "values" and i % (2 * T) == 2 * T - 1:
                        u = i // T
                        dve.wait_ge(S["pv_filled"], i + 1)
                        V.tensor_copy(oT[0:OROWS, u, :], banks[2 + u % 2][0:OROWS, :]).then_inc(S["oT_by_dve"], 1)
                    elif step == "wo":
                        dve.wait_ge(S["att_filled"], att_fill(steps, step, i))
                        o = banks[(2 + i) % 4][:, 0:HEADS * (C + 1)].rearrange("p (h c) -> p h c", h=HEADS)
                        chain(V.reciprocal(rden[:, i, :], o[:, :, C]))
                        chain.settle()
                        if i >= 1:
                            add_head_1(i - 1)
                        chain(V.scalar_tensor_tensor(out=y[:, i, :], in0=o[:, 0, 0:C], scalar=rden[:, i, 0:1], in1=bo_rows[:, :],
                                                     op0=ALU.mult, op1=ALU.add))
                        if i == T - 1:
                            chain.settle()
                            add_head_1(i)
                    elif step == "xt":
                        V.tensor_copy(xt[:, 4 * i:4 * i + 4, :].rearrange("p t n -> p (t n)"), filled("xt", i)[:, :]).then_inc(S["ffn_by_D"], 1)
                    elif step == "logits":
                        V.tensor_copy(lg[:, :], filled("logits")[:, 0:E]).then_inc(S["ffn_by_D"], 1)
                        dve.wait_ge(S["ffn_by_D"], evacuated_by("D", FILL_AT["logits"]))
                    elif step == "top2":
                        top2(chain, i)
                    elif step in ("route", "droute"):
                        bank = filled(step)
                        first = 0 if step == "route" else 2
                        V.tensor_scalar(ohA[:, :, :].rearrange("e k n -> e (k n)"), bank[:, 0:2 * P], unscale[:, first:first + 1], None, ALU.mult)
                        V.tensor_scalar(ohB[:, :, :].rearrange("e k n -> e (k n)"), bank[:, 0:2 * P], unscale[:, first + 1:first + 2], None, ALU.mult)
                        n = G if step == "route" else P
                        V.tensor_copy(pb[:, 0:n], bank[:, 2 * P:2 * P + n]).then_inc(S["ffn_by_D"], 1)
                        dve.wait_ge(S["ffn_by_D"], evacuated_by("D", FILL_AT[step]))
                    elif step in ("gather_b", "gather_a", "dgather_a", "dgather_b"):
                        if FILL_BY[FILL_AT[step] + i] == "D":
                            evacuate_gather(dve, "D", V.tensor_copy, step, i, gb if step in ("gather_b", "dgather_a") else ga)
                    elif step == "xbd" and i % 2 == 0:
                        V.tensor_copy(*x_block(2 * i + 1)).then_inc(S["xbd_by_dve"], 1)
                    elif step == "stage1":
                        V.tensor_tensor(tok[:, 8 * i:8 * i + 8, :], filled("stage1", i)[:, :].rearrange("q (g p) -> q g p", g=8),
                                        pb[:, 8 * i:8 * i + 8].unsqueeze(2).broadcast_to([P, 8, F1]), ALU.mult).then_inc(S["ffn_by_D"], 1)
                    elif step == "stage2" and i >= 1:
                        V.tensor_tensor(tok[:, 8 * i - 8:8 * i, :], filled("stage2", i - 1)[:, :].rearrange("q (g p) -> q g p", g=8),
                                        bup[:, :].unsqueeze(1).broadcast_to([P, 8, F1]), ALU.add).then_inc(S["ffn_by_D"], 1)
                    elif step == "dlogits" and i == 7:
                        for h in range(2):
                            V.tensor_copy(lg[G * h:G * h + G, :], filled("dlogits", h)[G * h:G * h + G, 0:E]).then_inc(S["ffn_by_D"], 1)
                        dve.wait_ge(S["ffn_by_D"], evacuated_by("D", FILL_AT["dlogits"] + 1))
                    elif step == "dstage1" and i >= 1:
                        V.tensor_tensor(tok[:, 8 * i - 8:8 * i, :].rearrange("q g (k o) -> q g k o", k=2),
                                        filled("dstage1", i - 1)[:, :].rearrange("q (g k o) -> q g k o", g=8, k=2),
                                        pb[:, :].rearrange("q (k g) -> q g k", k=2)[:, 8 * i - 8:8 * i].unsqueeze(3).broadcast_to([P, 8, 2, D1]),
                                        ALU.mult).then_inc(S["ffn_by_D"], 1)
                meet(dve, "dve")

            iterations(dve, run)

        @block.tensor
        def _(pe):
            M = nc.tensor.matmul
            pe.wait_ge(s_attw, 96)
            open_banks = {}

            def begin(stage, i=0):
                fill = FILL_AT[stage] + i
                if fill >= 4:
                    evacuated(fill - 4)
                return banks[4 + fill % 4]

            def evacuated(fill):
                for who in "AD":
                    if evacuated_by(who, fill):
                        pe.wait_ge(S[f"ffn_by_{who}"], evacuated_by(who, fill))

            def gather(stage, i, table, hot):
                bank = begin(stage, i)
                if stage[0] == "d":
                    for e in range(4):
                        for h in range(2):
                            last = M(bank[G * h:G * h + G, e * P:(e + 1) * P], table[:, (4 * i + e) * F1:(4 * i + e + 1) * F1],
                                     hot[:, :, G * h:G * h + G], start=True, stop=True)
                else:
                    for e in range(8):
                        for c in range(4):
                            last = M(bank[32 * c:32 * c + 32, e * G:(e + 1) * G], table[:, (8 * i + e) * D1:(8 * i + e + 1) * D1],
                                     hot[:, c % 2, G * (c // 2):G * (c // 2) + G], start=True, stop=True)
                last.then_inc(S["ffn_filled"], 1)

            def per_token(stage, s, left, right):
                if s < 8:
                    open_banks[s] = begin(stage, s)
                for g in range(8):
                    if s < 8:
                        M(open_banks[s][0:G, g * F1:(g + 1) * F1], left[0:G, 8 * s + g, :], right[0:G, 8 * s + g, :], start=True, stop=True)
                    if s >= 1:
                        last = M(open_banks[s - 1][G:P, g * F1:(g + 1) * F1], left[G:P, 8 * s - 8 + g, :], right[G:P, 8 * s - 8 + g, :],
                                 start=True, stop=True)
                if s >= 1:
                    last.then_inc(S["ffn_filled"], 1)

            def run(b, steps):
                if steps is FIRST:
                    pe.wait_ge(s_ffnw, 80)
                    pe.wait_ge(s_tabs, 1)
                for step, i in steps:
                    if step == "xnT":
                        if i == 0:
                            pe.wait_ge(S["norm_applied"], norm_count(steps, "norm1"))
                            if ("scores", 0) in steps:
                                pe.wait_ge(S["probs_ready"], UNITS * T)
                        for t in range(4):
                            last = nc.tensor.transpose(banks[i][:, P * t:P * t + P], xn[:, 4 * i + t, :], ident)
                        last.then_inc(S["att_filled"], 1)
                    elif step == "qkv":
                        if i == 0:
                            pe.wait_ge(S["xnT_by_act"], 1)
                            pe.wait_ge(S["xnT_by_dve"], 1)
                        if i >= 4:
                            pe.wait_ge(S["qkv_ready"], i - 3)
                        elif ("wo", 0) in steps:
                            pe.wait_ge(S["y_rows"], 5 + i)
                        M(banks[(2 + i) % 4][:, 0:3 * C], xnT[:, i * P:(i + 1) * P], wqkv[:, :], start=True, stop=True)\
                            .then_inc(S["att_filled"], 1)
                    elif step == "qkT":
                        array, h, half = QKT[i]
                        if i == 0:
                            pe.wait_ge(S["split_ready"], 1)
                        elif i == 4:
                            pe.wait_ge(S["split_ready"], 2)
                            pe.wait_ge(S["high_ready"], 3)
                        if i >= 4:
                            pe.wait_ge(S["qkT_by_act"] if i % 2 == 0 else S["qkT_by_dve"], (i - 4) // 2 + 1)
                        at = {"k": 2 * h, "q": 4 + 3 * h, "q_swapped": 5 + 3 * h}[array] * DH
                        for t in range(4):
                            last = M(banks[(2 + i) % 4][:, P * t:P * t + P], split[:, 4 * half + t, at:at + P], ident16[:, :], start=True, stop=True)
                        last.then_inc(S["att_filled"], 1)
                    elif step == "scores":
                        u, kt = divmod(i, T)
                        h, qh = divmod(u, QH)
                        if i >= 2:
                            pe.wait_ge(S["probs_ready"], i - 1)
                        for part, queries in enumerate((qT, qT_swapped)):
                            last = M(banks[kt % 2][:, :], kT[:, h, kt * P:(kt + 1) * P], queries[:, h, qh * BANK:(qh + 1) * BANK],
                                     start=(part == 0), stop=(part == 1))
                        last.then_inc(S["scores_filled"], 1)
                    elif step == "values":
                        u, kt = divmod(i, T)
                        h = u // QH
                        if kt == 0 and u >= 2:
                            pe.wait_ge(S["oT_by_act"] if u % 2 == 0 else S["oT_by_dve"], u // 2)
                        pe.wait_ge(S["probs_ready"], i + 1)
                        M(banks[2 + u % 2][0:OROWS, :], vv[:, kt * (OROWS + DH) + h * DH:kt * (OROWS + DH) + h * DH + OROWS], pT[:, u % 2, kt, :],
                          start=(kt == 0), stop=(kt == T - 1)).then_inc(S["pv_filled"], 1)
                    elif step == "wo":
                        if i == 0:
                            pe.wait_ge(S["oT_by_act"], UNITS // 2)
                            pe.wait_ge(S["oT_by_dve"], UNITS // 2)
                        if i in (2, 3) and ("xnT", 0) in steps:
                            pe.wait_ge(S["xnT_by_act"] if i == 2 else S["xnT_by_dve"], 1)
                        if i >= 4:
                            pe.wait_ge(S["y_rows"], i - 3)
                        for h in range(HEADS):
                            last = M(banks[(2 + i) % 4][:, h * (C + 1):(h + 1) * (C + 1)], oT[0:OROWS, h * QH + i // 4, (i % 4) * P:(i % 4 + 1) * P],
                                     wo[:, h, :], start=True, stop=True)
                        last.then_inc(S["att_filled"], 1)
                    elif step == "xt":
                        bank = begin("xt", i)
                        for t in range(4):
                            last = nc.tensor.transpose(bank[:, P * t:P * t + P], x2n[:, 4 * i + t, :], ident)
                        last.then_inc(S["ffn_filled"], 1)
                    elif step == "logits":
                        evacuated(FILL_AT["xt"] + 1)
                        bank = begin("logits")
                        for t in range(T):
                            last = M(bank[:, 0:E], xt[:, t, :], wup[:, t, :], start=(t == 0), stop=(t == T - 1))
                        last.then_inc(S["ffn_filled"], 1)
                    elif step in ("route", "droute"):
                        pe.wait_ge(S["route_ready"], 1 if step == "route" else 2)
                        bank = begin(step)
                        for k in range(2):
                            nc.tensor.transpose(bank[:, k * P:(k + 1) * P], oh[:, k, :], ident)
                        if step == "route":
                            last = M(bank[:, 2 * P:2 * P + G], spread[:, 0:P], mask_g, start=True, stop=True)
                        else:
                            last = M(bank[:, 2 * P:3 * P], mask_half, spread[:, 0:P], start=True, stop=True)
                        last.then_inc(S["ffn_filled"], 1)
                    elif step in ("gather_b", "dgather_a"):
                        if i == 0:
                            evacuated(FILL_AT["route" if step == "gather_b" else "droute"])
                        gather(step, i, *((tab[1], ohB) if step == "gather_b" else (tab[2], ohA)))
                    elif step in ("gather_a", "dgather_b"):
                        gather(step, i, *((tab[0], ohA) if step == "gather_a" else (tab[3], ohB)))
                    elif step == "stage1":
                        if i == 0:
                            evacuated(FILL_AT["gather_b"] + 7)
                            pe.wait_ge(S["xbd_by_act"], 8)
                            pe.wait_ge(S["xbd_by_dve"], 4)
                            pe.wait_ge(S["xbd_by_pool"], 4)
                        bank = begin("stage1", i)
                        for g in range(8):
                            last = M(bank[:, g * F1:(g + 1) * F1], xbd[:, 8 * i + g, :], gb[:, 8 * i + g, :], start=True, stop=True)
                        last.then_inc(S["ffn_filled"], 1)
                    elif step == "stage2":
                        if i == 0:
                            evacuated(FILL_AT["gather_a"] + 7)
                        per_token(step, i, ga, tok)
                    elif step == "dlogits":
                        if i == 0:
                            pe.wait_ge(S["hidden_ready"], 8)
                            for h in range(2):
                                open_banks[h] = begin(step, h)
                        for p in range(8 * i, 8 * i + 8):
                            for h in range(2):
                                last = M(open_banks[h][G * h:G * h + G, 0:E], tok[G * h:G * h + G, :, p], wdn[G * h:G * h + G, p, :],
                                         start=(p == 0), stop=(p == F1 - 1))
                                if p == F1 - 1:
                                    last.then_inc(S["ffn_filled"], 1)
                    elif step == "dstage1":
                        if i == 0:
                            evacuated(FILL_AT["dgather_b"] + 7)
                        per_token(step, i, tok, gb)
                    elif step == "dstage2":
                        if i == 0:
                            evacuated(FILL_AT["dstage1"] + 7)
                            for h in range(2):
                                open_banks[h] = begin(step, h)
                        for g in range(8 * i, 8 * i + 8):
                            for h in range(2):
                                for k in range(2):
                                    last = M(open_banks[h][32 * (g % 4):32 * (g % 4) + 32, (g // 4) * D1:(g // 4 + 1) * D1],
                                             tok[G * h:G * h + G, g, k * D1:(k + 1) * D1], ga[G * h:G * h + G, g, k * D1:(k + 1) * D1],
                                             start=(k == 0), stop=(k == 1))
                                if g == G - 1:
                                    last.then_inc(S["ffn_filled"], 1)
                meet(pe, "pe")

            iterations(pe, run)


def kernel(L0_attn_x, L0_attn_Wq, L0_attn_Wk, L0_attn_Wv, L0_attn_Wo, L0_attn_bo, L0_attn_ln_g, L0_attn_ln_b,
           L0_attn_q_gamma, L0_attn_k_gamma, L0_ffn_W_up, L0_ffn_A_up, L0_ffn_B_up, L0_ffn_scale_up, L0_ffn_bias_up,
           L0_ffn_W_down, L0_ffn_A_down, L0_ffn_B_down, L0_ffn_scale_down, L0_ffn_bias_down):
    import concourse.bacc as bacc
    from concourse.bass_utils import run_bass_kernel_spmd

    a = {k: np.asarray(v) for k, v in locals().items() if k.startswith("L0_")}

    def rows(v):
        return np.ascontiguousarray(np.broadcast_to(v.reshape(1, -1), (P, v.size)))

    n = np.arange(P)
    shape_consts = np.concatenate([
        np.eye(P), np.broadcast_to(n % E, (P, P)), (n[:, None] // G == n[None, :] // G),
        (n[:, None] % G == np.arange(G)[None, :]), -(n[:, None] >= E).astype(float)], axis=1).astype(np.float32)
    w_down = a["L0_ffn_W_down"].reshape(E, F1, F1).transpose(1, 2, 0)
    bias_up = a["L0_ffn_bias_up"].reshape(F1, F1)
    w_o = np.zeros((OROWS, HEADS, C + 1), np.float32)
    w_o[0:DH, 0, 0:C], w_o[ONES:OROWS, 1, 0:C] = a["L0_attn_Wo"].T[0:DH], a["L0_attn_Wo"].T[DH:C]
    w_o[DH, 0, C] = w_o[0, 1, C] = 1.0
    ins = {
        "x": a["L0_attn_x"],
        "w_qkv": np.concatenate([a["L0_attn_Wq"].T, a["L0_attn_Wk"].T, a["L0_attn_Wv"].T], axis=1),
        "w_o": w_o,
        "bo": rows(a["L0_attn_bo"]),
        "ln_affine": np.stack([a["L0_attn_ln_g"], a["L0_attn_ln_b"]], axis=1),
        "gammas": np.stack([rows(np.tile(a[k], HEADS)) for k in ("L0_attn_q_gamma", "L0_attn_k_gamma")], axis=1),
        "a_up": a["L0_ffn_A_up"].reshape(E, -1),
        "b_up": a["L0_ffn_B_up"].reshape(E, -1),
        "a_down": a["L0_ffn_A_down"].reshape(E, -1),
        "b_down": a["L0_ffn_B_down"].reshape(E, -1),
        "w_up": a["L0_ffn_W_up"].reshape(E, T, C).transpose(2, 1, 0),
        "w_down": np.concatenate([w_down, w_down], axis=0),
        "bias_up": np.concatenate([bias_up, bias_up], axis=0),
        "bias_down": rows(a["L0_ffn_bias_down"]),
        "scales": np.concatenate([rows(a["L0_ffn_scale_up"]), rows(a["L0_ffn_scale_down"])], axis=1),
        "shape_consts": shape_consts,
    }
    ins = {k: np.ascontiguousarray(v) for k, v in ins.items()}
    nc = bacc.Bacc("TRN2", target_bir_lowering=False, num_devices=1)
    h = {k: nc.dram_tensor(f"in_{k}", v.shape, mybir.dt.from_np(v.dtype), kind="ExternalInput").ap() for k, v in ins.items()}
    out = nc.dram_tensor("out", (B, N, C), F32, kind="ExternalOutput").ap()
    tables = [h.pop(k) for k in ("a_up", "b_up", "a_down", "b_down")]
    build_program(nc, tables=tables, out=out, **h)
    r = run_bass_kernel_spmd(nc, [{f"in_{k}": v for k, v in ins.items()}], core_ids=[0])
    return r.results[0]["out"]
```
